# Optimizing a Trainium2 kernel written in Bass

```python
import numpy as np
import jax
import jax.numpy as jnp

def _softmax(x, axis=-1):
    return jax.nn.softmax(x, axis=axis)

def _gelu(x):
    return jax.nn.gelu(x, approximate=True)

def _silu(x):
    return jax.nn.silu(x)

def _sigmoid(x):
    return jax.nn.sigmoid(x)

def _layernorm(x, axis=-1, eps=1e-05):
    m = jnp.mean(x, axis=axis, keepdims=True)
    v = jnp.var(x, axis=axis, keepdims=True)
    return (x - m) / jnp.sqrt(v + eps)

def _scatter_add(tgt, idx, src, axis=0):
    return tgt.at[idx].add(src)

def _segment_sum(src, seg, n):
    return jax.ops.segment_sum(src, seg, n)
kernel_name = 'mk_gnn_resnorm_d2_gnn_r8_f3b360'

def setup_inputs(seed: int=0):
    np.random.seed(seed)
    _w = jnp.asarray

    def _rec_inputs():
        import jax
        import jax.numpy as jnp
        _gk = jax.random.key(seed)
        x = -0.0005121 + 1.001 * jax.random.normal(jax.random.fold_in(_gk, 1), (12500, 64), jnp.float32)
        src = jax.random.randint(jax.random.fold_in(_gk, 2), (200000,), 0, 12500, jnp.int32)
        dst = jnp.minimum((12500 * jax.random.uniform(jax.random.fold_in(_gk, 3), (200000,)) ** 2.0).astype(jnp.int32), 99999)
        _o = jnp.argsort(dst, stable=True)
        src = src[_o]
        dst = dst[_o]
        edge_attr_32 = 0.000196303 + 1.00016 * jax.random.normal(jax.random.fold_in(_gk, 13), (200000, 32), jnp.float32)
        return (x, src, dst, edge_attr_32)
    x, src, dst, edge_attr_32 = _rec_inputs()

    def _L0_gnn_setup():
        import jax, jax.numpy as jnp
        import numpy as np
        N_NODES = 6250
        N_EDGES = 200000
        D_IN = 64
        D_OUT = 64
        K_HOPS = 2
        key = jax.random.key(seed)
        k1, k2, k3, k4, k5 = jax.random.split(key, 5)
        feat = jax.random.normal(k1, (N_NODES, D_IN), dtype=jnp.float32)
        weight = jax.random.normal(k2, (D_OUT, D_IN * (K_HOPS + 1)), dtype=jnp.float32) * 0.05
        bias = jax.random.normal(k3, (D_OUT,), dtype=jnp.float32) * 0.05
        src = jax.random.randint(k4, (N_EDGES,), 0, N_NODES, dtype=jnp.int64)
        dst = jax.random.randint(k5, (N_EDGES,), 0, N_NODES, dtype=jnp.int64)
        return {'feat': feat, 'weight': weight, 'bias': bias, 'src': src, 'dst': dst}
    _L0_gnn_all = _L0_gnn_setup()
    _L0_gnn_in = {k: v for k, v in _L0_gnn_all.items() if k in ('weight', 'bias')}
    del _L0_gnn_all

    def _L1_gnn_setup():
        import jax, jax.numpy as jnp
        import numpy as np
        N, E, G = (6250, 100000, 16)
        F_X, F_E, F_U = (64, 32, 64)
        H1, H2, H3 = (128, 64, 64)

        def _lin_init(key, fan_in, fan_out):
            kw, kb = jax.random.split(key)
            bound = 1.0 / np.sqrt(fan_in)
            W = jax.random.uniform(kw, (fan_in, fan_out), jnp.float32, -bound, bound)
            b = jax.random.uniform(kb, (fan_out,), jnp.float32, -bound, bound)
            return (W, b)
        key = jax.random.key(seed)
        ks = jax.random.split(key, 9)
        x = jax.random.normal(ks[0], (N, F_X), jnp.float32)
        edge_index = jax.random.randint(ks[1], (2, E), 0, N, jnp.int32)
        edge_attr = jax.random.normal(ks[2], (E, F_E), jnp.float32)
        u = jax.random.normal(ks[3], (G, F_U), jnp.float32)
        batch = jnp.sort(jax.random.randint(ks[4], (N,), 0, G, jnp.int32))
        W1, b1 = _lin_init(ks[5], F_X + F_E, H1)
        W2, b2 = _lin_init(ks[6], H1, H2)
        W3, b3 = _lin_init(ks[7], H2 + F_X + F_U, H2)
        W4, b4 = _lin_init(ks[8], H2, H3)
        return {'x': x, 'edge_index': edge_index, 'edge_attr': edge_attr, 'u': u, 'batch': batch, 'W1': W1, 'b1': b1, 'W2': W2, 'b2': b2, 'W3': W3, 'b3': b3, 'W4': W4, 'b4': b4}
    _L1_gnn_all = _L1_gnn_setup()
    _L1_gnn_in = {k: v for k, v in _L1_gnn_all.items() if k in ('u', 'W1', 'b1', 'W2', 'b2', 'W3', 'b3', 'W4', 'b4')}
    del _L1_gnn_all
    return {'x': x, 'src': src, 'dst': dst, 'edge_attr_32': edge_attr_32, 'L0_gnn_weight': _L0_gnn_in['weight'], 'L0_gnn_bias': _L0_gnn_in['bias'], 'L1_gnn_u': _L1_gnn_in['u'], 'L1_gnn_W1': _L1_gnn_in['W1'], 'L1_gnn_b1': _L1_gnn_in['b1'], 'L1_gnn_W2': _L1_gnn_in['W2'], 'L1_gnn_b2': _L1_gnn_in['b2'], 'L1_gnn_W3': _L1_gnn_in['W3'], 'L1_gnn_b3': _L1_gnn_in['b3'], 'L1_gnn_W4': _L1_gnn_in['W4'], 'L1_gnn_b4': _L1_gnn_in['b4']}

def reference(x, src, dst, edge_attr_32, L0_gnn_weight, L0_gnn_bias, L1_gnn_u, L1_gnn_W1, L1_gnn_b1, L1_gnn_W2, L1_gnn_b2, L1_gnn_W3, L1_gnn_b3, L1_gnn_W4, L1_gnn_b4):
    import jax
    import jax.numpy as jnp

    def _L0_gnn_ref(feat, weight, bias, src, dst):
        import jax, jax.numpy as jnp
        import numpy as np
        N_NODES = 6250
        N_EDGES = 200000
        D_IN = 64
        D_OUT = 64
        K_HOPS = 2
        n = feat.shape[0]
        deg = jax.ops.segment_sum(jnp.ones_like(dst, dtype=feat.dtype), dst, num_segments=n)
        norm = jax.lax.rsqrt(jnp.maximum(deg, 1.0))[:, None]
        fstack = [feat]
        h = feat
        for _ in range(K_HOPS):
            h = h * norm
            h = jax.ops.segment_sum(h[src], dst, num_segments=n)
            h = h * norm
            fstack.append(h)
        out = jnp.concatenate(fstack, axis=-1) @ weight.T + bias
        return out

    def _L1_gnn_ref(x, edge_index, edge_attr, u, batch, W1, b1, W2, b2, W3, b3, W4, b4):
        import jax, jax.numpy as jnp
        import numpy as np
        N, E, G = (6250, 100000, 16)
        F_X, F_E, F_U = (64, 32, 64)
        H1, H2, H3 = (128, 64, 64)

        def _lin_init(key, fan_in, fan_out):
            kw, kb = jax.random.split(key)
            bound = 1.0 / np.sqrt(fan_in)
            W = jax.random.uniform(kw, (fan_in, fan_out), jnp.float32, -bound, bound)
            b = jax.random.uniform(kb, (fan_out,), jnp.float32, -bound, bound)
            return (W, b)
        row, col = (edge_index[0], edge_index[1])
        e = jnp.concatenate([x[row], edge_attr], axis=1)
        e = jax.nn.relu(e @ W1 + b1) @ W2 + b2
        s = jax.ops.segment_sum(e, col, num_segments=x.shape[0])
        cnt = jax.ops.segment_sum(jnp.ones((e.shape[0],), e.dtype), col, num_segments=x.shape[0])
        agg = s / jnp.maximum(cnt, 1.0)[:, None]
        h = jnp.concatenate([x, agg, u[batch]], axis=1)
        return jax.nn.relu(h @ W3 + b3) @ W4 + b4
    edge_index = jnp.stack([src, dst])
    batch0 = jnp.zeros((12500,), jnp.int32)
    x = _layernorm(x + _L0_gnn_ref(x, L0_gnn_weight, L0_gnn_bias, src, dst), axis=-1)
    x = _layernorm(x + _L1_gnn_ref(x, edge_index, edge_attr_32, L1_gnn_u, batch0, L1_gnn_W1, L1_gnn_b1, L1_gnn_W2, L1_gnn_b2, L1_gnn_W3, L1_gnn_b3, L1_gnn_W4, L1_gnn_b4), axis=-1)
    return x

_drawn_inputs = setup_inputs


def setup_inputs(seed=0):
    import zlib

    import numpy as np

    out = dict(_drawn_inputs(seed))
    spreads = {}
    factors = {'edge_attr_32': 8.0,
     'L1_gnn_W1': 7.479,
     'L1_gnn_b1': 8.0,
     'L1_gnn_W2': 3.692,
     'L1_gnn_b2': 21.629,
     'L1_gnn_b3': 3.336}
    for name, (base, spread) in spreads.items():
        noise = np.random.default_rng([zlib.crc32(name.encode()), seed]).standard_normal(out[name].shape)
        drawn = base * np.exp(spread * noise) if base else spread * noise
        out[name] = jnp.asarray(drawn.astype(out[name].dtype))
    for name, factor in factors.items():
        out[name] = (out[name] * factor).astype(out[name].dtype)
    return out
```

```python
from contextlib import ExitStack

import concourse.bass as bass
from concourse import mybir

ALU = mybir.AluOpType
ACT = mybir.ActivationFunctionType
AX = mybir.AxisListType
F32 = mybir.dt.float32
BF16 = mybir.dt.bfloat16
I32 = mybir.dt.int32

P = 128
EPS = 1e-5


class Plan:

    def __init__(self, nodes, edges, feat, edge_feat, hidden):
        self.N, self.E, self.D, self.FE, self.H = nodes, edges, feat, edge_feat, hidden
        self.NB = 100
        self.NP = nodes // self.NB
        assert self.NP * self.NB == nodes and self.NP <= P
        self.TG = 4
        self.GB = 8
        self.TH = self.TG * self.GB // 2
        per_turn = P * self.TG * self.GB
        self.TURNS = -(-edges // per_turn)
        self.T = self.TURNS * self.TG * self.GB
        self.G = self.TURNS * self.GB
        self.WIN = 128
        self.CB = 8


def ds(start, size):
    return bass.ds(start, size)


def wait(engine, semaphore, value):
    if not isinstance(value, int) or value > 0:
        engine.wait_ge(semaphore, value)


def wait_apart(engine, semaphore, value, passed):
    if not isinstance(value, int):
        engine.wait_ge(semaphore, value)
        engine.sem_inc(passed, 1)
    elif value > 0:
        engine.wait_ge(semaphore, value)


def prologue(nc, plan, mem, io):
    N, D, NB, NP, T, G, TG = plan.N, plan.D, plan.NB, plan.NP, plan.T, plan.G, plan.TG
    U = 8
    GC = G // 4
    with ExitStack() as ctx:
        sb = lambda n, s, d: ctx.enter_context(nc.sbuf_tensor(n, s, d))
        ps = lambda n, s, d: ctx.enter_context(nc.psum_tensor(n, s, d))
        sem = lambda n: ctx.enter_context(nc.semaphore(n))
        dst_i = sb("dst_i", [P, T], I32)
        dst_f = sb("dst_f", [P, T], F32)
        hi_i = sb("hi_i", [P, T], I32)
        digit_hi = sb("digit_hi", [P, T], F32)
        digit_lo = sb("digit_lo", [P, T], F32)
        fix = sb("fix", [P, T], F32)
        hi_b = sb("hi_b", [P, T], BF16)
        lo_b = sb("lo_b", [P, T], BF16)
        iota_i = sb("iota_i", [P, P], I32)
        iota_b = sb("iota_b", [P, P], BF16)
        one_hi = sb("one_hi", [P, 4, U, NP], BF16)
        one_lo = sb("one_lo", [P, 4, U, NB], BF16)
        deg = sb("deg", [NP, NB], F32)
        tmp = sb("tmp", [NP, NB], F32)
        tmp2 = sb("tmp2", [NP, NB], F32)
        least = sb("least", [P, G], F32)
        least_t = sb("least_t", [GC, 4], F32)
        least_i = sb("least_i", [GC, 4], I32)
        base_bc = sb("base_bc", [P, G], F32)
        base_bi = sb("base_bi", [P, G], I32)
        far = sb("far", [P, 1], F32)
        far_1 = sb("far_1", [1, 1], F32)
        far_i = sb("far_i", [1, 1], I32)
        deg_ps = ps("deg_ps", [NP, 512], F32)
        tr_ps = ps("tr_ps", [P, 512], F32)

        loaded = sem("p_loaded")
        iota_ready = sem("p_iota")
        dve = sem("p_dve")
        hot_ready = sem("p_hot_ready")
        hot_used = sem("p_hot_used")
        turned = sem("p_turned")
        scaled = sem("p_sqrt")
        spread = sem("p_spread")
        table_out = sem("p_table_out")
        x_loaded = sem("p_x_loaded")
        w_loaded = sem("p_w_loaded")
        marks = {}

        block = ctx.enter_context(nc.Block())

        @block.vector
        def _(v):
            count = [0]

            def link(ins, mark=None):
                count[0] += 1
                ins.then_inc(dve, 1)
                v.wait_ge(dve, count[0])
                if mark:
                    marks[mark] = count[0]

            v.wait_ge(iota_ready, 1)
            link(v.tensor_copy(iota_b[:], iota_i[:]))
            link(v.tensor_copy(mem["iota_f"][:], iota_i[:]))
            v.wait_ge(loaded, 16)
            link(v.tensor_copy(dst_f[:], dst_i[:]))
            link(v.tensor_scalar(digit_lo[:], dst_f[:], 1.0 / NB, 0.5 / NB - 0.5, ALU.mult, ALU.add))
            link(v.tensor_copy(hi_i[:], digit_lo[:]))
            link(v.tensor_copy(digit_hi[:], hi_i[:]))
            link(v.scalar_tensor_tensor(out=digit_lo[:], in0=digit_hi[:], scalar=-float(NB), in1=dst_f[:], op0=ALU.mult, op1=ALU.add))
            link(v.tensor_scalar(fix[:], digit_lo[:], float(NB), None, ALU.is_ge))
            link(v.tensor_tensor(hi_b[:], digit_hi[:], fix[:], ALU.add))
            link(v.scalar_tensor_tensor(out=lo_b[:], in0=fix[:], scalar=-float(NB), in1=digit_lo[:], op0=ALU.mult, op1=ALU.add))

            def hot(n, k):
                wait(v, hot_used, n - 3)
                at = ds(n * U, U) if not isinstance(n, int) else slice(n * U, n * U + U)
                v.tensor_tensor(one_hi[:, k], hi_b[:, at].unsqueeze(2).broadcast_to([P, U, NP]),
                                iota_b[:, 0:NP].unsqueeze(1).broadcast_to([P, U, NP]), ALU.is_equal)
                v.tensor_tensor(one_lo[:, k], lo_b[:, at].unsqueeze(2).broadcast_to([P, U, NB]),
                                iota_b[:, 0:NB].unsqueeze(1).broadcast_to([P, U, NB]), ALU.is_equal).then_inc(hot_ready, 1)

            for k in range(4):
                hot(k, k)
            with v.Fori(1, T // U // 4) as i:
                for k in range(4):
                    hot(i * 4 + k, k)
            link(v.tensor_reduce(least[:], dst_f[:].rearrange("p (g t) -> p g t", t=TG), AX.X, ALU.min), "least")

            v.wait_ge(hot_used, T // U)
            link(v.tensor_copy(deg[:], deg_ps[:, 0:NB]))
            link(v.tensor_scalar(tmp[:], deg[:], 1.0, None, ALU.max), "deg_max")
            link(v.reciprocal(mem["inv"][:], tmp[:]))
            link(v.tensor_tensor(mem["some"][:], deg[:], mem["inv"][:], ALU.mult))
            v.wait_ge(scaled, 1)
            link(v.reciprocal(mem["norm"][:], tmp2[:]))
            link(v.tensor_tensor(tmp2[:], mem["norm"][:], mem["norm"][:], ALU.mult))
            link(v.tensor_tensor(tmp2[:], tmp2[:], tmp[:], ALU.mult))
            link(v.tensor_scalar(tmp2[:], tmp2[:], -0.5, 1.5, ALU.mult, ALU.add))
            link(v.tensor_tensor(mem["norm"][:], tmp2[:], mem["norm"][:], ALU.mult))
            link(v.tensor_tensor(mem["norm2"][:], mem["norm"][:], mem["norm"][:], ALU.mult))
            v.wait_ge(x_loaded, 16)
            link(v.tensor_tensor(mem["stage"][0:NP, 0:NB * D].rearrange("p (b d) -> p b d", d=D),
                                 mem["xr"][:].rearrange("p (b d) -> p b d", d=D),
                                 mem["norm"][:].unsqueeze(2).broadcast_to([NP, NB, D]), ALU.mult), "table")

            v.wait_ge(turned, 1)
            link(v.tensor_reduce(least_t[:], tr_ps[0:GC, :].rearrange("q (c p) -> q c p", p=P), AX.X, ALU.min))
            link(v.tensor_copy(least_i[:], least_t[:]), "least_i")
            v.wait_ge(spread, 48)
            link(v.tensor_copy(base_bc[:], base_bi[:]))
            link(v.tensor_tensor(mem["rel0"][:].rearrange("p (g t) -> p g t", t=TG), dst_f[:].rearrange("p (g t) -> p g t", t=TG),
                                 base_bc[:].unsqueeze(2).broadcast_to([P, G, TG]), ALU.subtract))
            link(v.tensor_reduce(far[:], mem["rel0"][:], AX.X, ALU.max), "far")
            v.wait_ge(turned, 2)
            link(v.tensor_reduce(far_1[:], tr_ps[0:1, 0:P], AX.X, ALU.max))
            link(v.tensor_copy(far_i[:], far_1[:]))
            link(v.tensor_scalar(far_i[:], far_i[:], 7, None, ALU.arith_shift_right))
            link(v.tensor_scalar(mem["passes"][:], far_i[:], 1, None, ALU.add))

        @block.sync
        def _(sp):
            sp.dma_start(dst_i[:], io["dst"]).then_inc(loaded, 16)
            sp.dma_start(mem["xr"][:], io["x"].rearrange("(p b) d -> p (b d)", b=NB)).then_inc(x_loaded, 16)
            for name in ("ident", "w0", "w12", "bias0", "w1x", "w1e", "b1", "w2", "b2", "w3xa", "w3u", "b3", "w4", "b4", "u0"):
                sp.dma_start(mem[name][:], io[name]).then_inc(w_loaded, 16)
            sp.wait_ge(dve, marks["least_i"])
            sp.dma_start(io["scratch_base"].rearrange("(q c) -> q c", c=4), least_i[:]).then_inc(spread, 16)
            sp.wait_ge(spread, 16)
            sp.dma_start(mem["base_row0"][:], io["scratch_base"].rearrange("(a g) -> a g", a=1)).then_inc(spread, 16)
            sp.dma_start(base_bi[:], io["scratch_base"].rearrange("(a g) -> a g", a=1).broadcast_to([P, G])).then_inc(spread, 16)
            sp.wait_ge(dve, marks["table"])
            sp.dma_start(io["table0"].rearrange("(p b) d -> p (b d)", b=NB), mem["stage"][0:NP, 0:NB * D]).then_inc(table_out, 16)
            sp.wait_ge(table_out, 16)
            sp.wait_ge(w_loaded, 16 * 15)
            sp.wait_ge(spread, 48)

        @block.gpsimd
        def _(pool):
            pool.iota(iota_i[:], [[1, P]], base=0, channel_multiplier=0).then_inc(iota_ready, 1)

        @block.scalar
        def _(act):
            act.wait_ge(dve, marks["deg_max"])
            act.activation(tmp2[:], tmp[:], ACT.Sqrt).then_inc(scaled, 1)

        @block.tensor
        def _(pe):
            first = [True]

            def turn(n, k, start, stop):
                pe.wait_ge(hot_ready, n + 1)
                for u in range(U):
                    mm = pe.matmul(deg_ps[:, 0:NB], one_hi[:, k, u, :], one_lo[:, k, u, :],
                                   start=start and u == 0, stop=stop and u == U - 1)
                mm.then_inc(hot_used, 1)

            n_hot = T // U
            for k in range(4):
                turn(k, k, k == 0, False)
            with pe.Fori(1, n_hot // 4 - 1) as i:
                for k in range(4):
                    turn(i * 4 + k, k, False, False)
            for k in range(4):
                turn(n_hot - 4 + k, k, False, k == 3)
            pe.wait_ge(w_loaded, 16 * 15)
            pe.wait_ge(dve, marks["least"])
            for c in range(4):
                tr = pe.transpose(tr_ps[0:GC, c * P:(c + 1) * P], least[:].rearrange("p (q c) -> p c q", c=4)[:, c, :], mem["ident"][:])
            tr.then_inc(turned, 1)
            pe.wait_ge(dve, marks["far"])
            pe.transpose(tr_ps[0:1, 0:P], far[:], mem["ident"][:]).then_inc(turned, 1)


def edge_sums(nc, plan, mem, io, tag, table, low, edge_mlp=False):
    N, D, T, G, TG, GB, TH, WIN, TURNS = plan.N, plan.D, plan.T, plan.G, plan.TG, plan.GB, plan.TH, plan.WIN, plan.TURNS
    F = plan.H if edge_mlp else D
    HG = GB // 2
    with ExitStack() as ctx:
        sb = lambda n, s, d: ctx.enter_context(nc.sbuf_tensor(tag + n, s, d))
        ps = lambda n, s, d: ctx.enter_context(nc.psum_tensor(tag + n, s, d))
        sem = lambda n: ctx.enter_context(nc.semaphore(tag + n))
        index = sb("index", [P, 2, TH], I32)
        rows = sb("rows", [P, GB, TG, F], F32)
        hot = sb("hot", [P, 4, TG, WIN], F32)
        rel = sb("rel", [P, T], F32)
        base = sb("base", [1, G], I32)
        seg_ps = [ps(f"seg_ps{k}", [P, 512], F32) for k in range(2)]
        if edge_mlp:
            edges = sb("edges", [plan.FE, 2, TH * P], F32)
            pre = sb("pre", [P, 2, TG, F], F32)
            hid = sb("hid", [P, 2, TG, F], F32)
            emb_ps = [ps(f"emb_ps{k}", [P, 512], F32) for k in range(2)]

        index_in = [sem(f"index_in{h}") for h in range(2)]
        rows_in = [sem(f"rows_in{k}") for k in range(GB)]
        hot_ready = sem("hot_ready")
        seg_done = sem("seg_done")
        sum_done = sem("sum_done")
        if edge_mlp:
            edges_in = [sem(f"edges_in{h}") for h in range(2)]
            emb_done = sem("emb_done")
            pre_ready = sem("pre_ready")
            hid_ready = sem("hid_ready")
        start = sem("start")
        pass_done = sem("pass_done")
        moved = sem("moved")
        passed = sem("passed")

        block = ctx.enter_context(nc.Block())

        def passes(engine, turn, last=None, after=None):
            n = engine.value_load(mem["passes"][0:1, 0:1], min_val=1, max_val=-(-N // WIN) + 1)
            with engine.Fori(0, n) as p:
                turn(0, p * TURNS)
                with engine.Fori(1, TURNS) as i:
                    turn(i, p * TURNS + i)
                if last:
                    last(TURNS - 1, p * TURNS + TURNS - 1)
                if after:
                    after(p)
                else:
                    wait_apart(engine, pass_done, p + 1, passed)

        def met(engine, semaphore, count, i, m, apart=False):
            if isinstance(i, int) and count(i) <= 0:
                return
            if apart:
                wait_apart(engine, semaphore, count(m), passed)
            else:
                engine.wait_ge(semaphore, count(m))

        @block.sync
        def _(sp):
            def turn(i, m):
                for h in range(2):
                    for k in range(h * HG, h * HG + HG):
                        met(sp, rows_in[k], lambda j: j * 16 * TG, i, m, apart=True)
                    sp.dma_start(index[:, h, :], io["src"][ds(i * 2 + h, 1)].rearrange("a p t -> (a p) t")).then_inc(index_in[h], 16)
                    if edge_mlp:
                        met(sp, emb_done, lambda j: j * GB - GB + (h + 1) * HG, i, m, apart=True)
                        sp.dma_start(edges[:, h, :], io["edge_t"][ds(i * 2 + h, 1)].rearrange("a f e -> (a f) e")).then_inc(edges_in[h], 16)

            passes(sp, turn)

        @block.gpsimd
        def _(pool):
            def turn(i, m):
                for h in range(2):
                    met(pool, index_in[h], lambda j: j * 16 + 16, i, m, apart=True)
                    for k in range(h * HG, h * HG + HG):
                        met(pool, pre_ready if edge_mlp else seg_done, lambda j: j * GB - GB + k + 1, i, m, apart=True)
                        for t in range(TG):
                            at = (k - h * HG) * TG + t
                            pool.indirect_dma_start(rows[:, k, t, :], None, table,
                                                    bass.IndirectOffsetOnAxis(ap=index[:, h, at:at + 1], axis=0)
                                                    ).then_inc(rows_in[k], 16)

            passes(pool, turn)

        if edge_mlp:
            @block.scalar
            def _(act):
                def turn(i, m):
                    for k in range(GB):
                        met(act, pre_ready, lambda j: j * GB + k + 1, i, m)
                        met(act, seg_done, lambda j: j * GB + k - 1, i, m)
                        act.activation(hid[:, k % 2], pre[:, k % 2], ACT.Relu).then_inc(hid_ready, 1)

                passes(act, turn)

        @block.tensor
        def _(pe):
            def embed(i, m, k):
                if k % HG == 0:
                    met(pe, edges_in[k // HG], lambda j: j * 16 + 16, i, m)
                met(pe, pre_ready, lambda j: j * GB + k - 1, i, m)
                for t in range(TG):
                    at = ((k % HG) * TG + t) * P
                    mm = pe.matmul(emb_ps[k % 2][:, t * F:(t + 1) * F], edges[:, k // HG, at:at + P], mem["w1e"][:],
                                   start=True, stop=True)
                mm.then_inc(emb_done, 1)

            def segment(i, m, k):
                met(pe, hot_ready, lambda j: j * GB + k + 1, i, m)
                if edge_mlp:
                    met(pe, hid_ready, lambda j: j * GB + k + 1, i, m)
                else:
                    met(pe, rows_in[k], lambda j: j * 16 * TG + 16 * TG, i, m)
                met(pe, sum_done, lambda j: j * GB + k - 1, i, m)
                for t in range(TG):
                    values = hid[:, k % 2, t, :] if edge_mlp else rows[:, k, t, :]
                    mm = pe.matmul(seg_ps[k % 2][low:low + F, 0:WIN], values, hot[:, k % 4, t, :], start=(t == 0), stop=(t == TG - 1))
                mm.then_inc(seg_done, 1)

            def turn(i, m):
                for k in range(GB):
                    if not edge_mlp:
                        segment(i, m, k)
                        continue
                    embed(i, m, k)
                    if k > 0 or not isinstance(i, int):
                        segment(i, m, k - 1)

            passes(pe, turn, last=(lambda i, m: segment(i, m, GB - 1)) if edge_mlp else None)

        @block.vector
        def _(v):
            v.memset(mem["sums"][low:low + F, :], 0.0).then_inc(start, 1)
            v.tensor_copy(rel[:], mem["rel0"][:]).then_inc(start, 1)
            v.tensor_copy(base[:], mem["base_row0"][:]).then_inc(start, 1)
            v.wait_ge(start, 3)

            def one_hot(i, m, k):
                met(v, seg_done, lambda j: j * GB + k - 3, i, m)
                v.tensor_tensor(hot[:, k % 4], rel[:, ds((i * GB + k) * TG, TG)].unsqueeze(2).broadcast_to([P, TG, WIN]),
                                mem["iota_f"][:, 0:WIN].unsqueeze(1).broadcast_to([P, TG, WIN]), ALU.is_equal).then_inc(hot_ready, 1)

            def add_parts(i, m, k):
                met(v, rows_in[k], lambda j: j * 16 * TG + 16 * TG, i, m)
                met(v, emb_done, lambda j: j * GB + k + 1, i, m)
                met(v, hid_ready, lambda j: j * GB + k - 1, i, m)
                v.tensor_tensor(pre[:, k % 2], emb_ps[k % 2][:].rearrange("p (t f) -> p t f", f=F), rows[:, k], ALU.add).then_inc(pre_ready, 1)

            def add_sums(i, m, k):
                first = v.value_load(base[0:1, ds(i * GB + k, 1)], min_val=0, max_val=N)
                met(v, seg_done, lambda j: j * GB + k + 1, i, m)
                met(v, sum_done, lambda j: j * GB + k, i, m)
                window = mem["sums"][low:low + F, ds(first, WIN)]
                v.tensor_tensor(window, window, seg_ps[k % 2][low:low + F, 0:WIN], ALU.add).then_inc(sum_done, 1)

            def turn(i, m):
                for k in range(GB):
                    one_hot(i, m, k)
                    if edge_mlp:
                        add_parts(i, m, k)
                    if k > 0 or not isinstance(i, int):
                        add_sums(i, m, k - 1)

            def after(p):
                v.wait_ge(sum_done, p * G + G)
                v.tensor_scalar(rel[:], rel[:], -float(WIN), None, ALU.add).then_inc(moved, 1)
                v.tensor_scalar(base[:], base[:], WIN, N, ALU.add, ALU.min).then_inc(moved, 1)
                v.wait_ge(moved, p * 2 + 2)
                v.sem_inc(pass_done, 1)

            passes(v, turn, last=lambda i, m: add_sums(i, m, GB - 1), after=after)


def chunks(plan):
    return plan.NB // plan.CB, plan.NB % plan.CB


def over_chunks(engine, plan, step):
    full, rest = chunks(plan)
    step(0, plan.CB)
    with engine.Fori(1, full) as c:
        step(c, plan.CB)
    if rest:
        step(full, rest)


def second_table(nc, plan, mem, io):
    D, NB, NP, CB = plan.D, plan.NB, plan.NP, plan.CB
    n_chunks = -(-NB // CB)
    with ExitStack() as ctx:
        sem = lambda n: ctx.enter_context(nc.semaphore("t_" + n))
        part = ctx.enter_context(nc.sbuf_tensor("t_part", [D, CB, NP], F32))
        rows_ps = ctx.enter_context(nc.psum_tensor("t_rows_ps", [P, 512], F32))
        picked, turned, scaled, out = sem("picked"), sem("turned"), sem("scaled"), sem("out")
        passed = sem("passed")
        block = ctx.enter_context(nc.Block())
        sums = mem["sums"][0:D, 0:plan.N].rearrange("f (p b) -> f b p", b=NB)
        stage = mem["stage"][0:NP, 0:NB * D].rearrange("p (b d) -> p b d", d=D)

        @block.scalar
        def _(act):
            def step(c, nb):
                wait(act, turned, c)
                act.copy(part[:, 0:nb, :], sums[:, ds(c * CB, nb), :]).then_inc(picked, 1)

            over_chunks(act, plan, step)

        @block.tensor
        def _(pe):
            def step(c, nb):
                wait(pe, scaled, c)
                wait_apart(pe, picked, c + 1, passed)
                for b in range(nb):
                    tr = pe.transpose(rows_ps[0:NP, b * D:(b + 1) * D], part[:, b, :], mem["ident"][0:D, 0:D])
                tr.then_inc(turned, 1)

            over_chunks(pe, plan, step)

        @block.vector
        def _(v):
            def step(c, nb):
                v.wait_ge(turned, c + 1)
                v.tensor_tensor(stage[:, ds(c * CB, nb), :], rows_ps[0:NP, 0:nb * D].rearrange("p (b d) -> p b d", d=D),
                                mem["norm2"][:, ds(c * CB, nb)].unsqueeze(2).broadcast_to([NP, nb, D]), ALU.mult).then_inc(scaled, 1)

            over_chunks(v, plan, step)

        @block.sync
        def _(sp):
            sp.wait_ge(scaled, n_chunks)
            sp.dma_start(io["table1"].rearrange("(p b) d -> p (b d)", b=NB), mem["stage"][0:NP, 0:NB * D]).then_inc(out, 16)
            sp.wait_ge(out, 16)


def layernorm(v, link, mem, t, sq, stat, out, nb, D, wait_sqrt, ask_sqrt, np_):
    wide = lambda a: a.unsqueeze(2).broadcast_to([np_, nb, D])
    s = lambda k: stat[:, k, 0:nb]
    link(v.tensor_reduce(s(0), t, AX.X, ALU.add))
    link(v.tensor_scalar(s(1), s(0), -1.0 / D, None, ALU.mult))
    link(v.tensor_tensor(t, t, wide(s(1)), ALU.add))
    link(v.tensor_tensor(sq, t, t, ALU.mult))
    link(v.tensor_reduce(s(2), sq, AX.X, ALU.add))
    link(v.tensor_scalar(s(3), s(2), 1.0 / D, EPS, ALU.mult, ALU.add))
    ask_sqrt()
    wait_sqrt()
    link(v.reciprocal(s(5), s(4)))
    link(v.tensor_tensor(s(6), s(5), s(5), ALU.mult))
    link(v.tensor_tensor(s(6), s(6), s(3), ALU.mult))
    link(v.tensor_scalar(s(6), s(6), -0.5, 1.5, ALU.mult, ALU.add))
    link(v.tensor_tensor(s(5), s(6), s(5), ALU.mult))
    return v.tensor_tensor(out, t, wide(s(5)), ALU.mult)


def first_layer(nc, plan, mem, io):
    N, D, H, NB, NP, CB = plan.N, plan.D, plan.H, plan.NB, plan.NP, plan.CB
    with ExitStack() as ctx:
        sb = lambda n, s: ctx.enter_context(nc.sbuf_tensor("f_" + n, s, F32))
        ps = lambda n: ctx.enter_context(nc.psum_tensor("f_" + n, [P, 512], F32))
        sem = lambda n: ctx.enter_context(nc.semaphore("f_" + n))
        part = sb("part", [P, CB, NP])
        x_t = sb("x_t", [D, CB, NP])
        x1_t = sb("x1_t", [D, CB, NP])
        acc, sq = sb("acc", [NP, CB, D]), sb("sq", [NP, CB, D])
        stat = sb("stat", [NP, 7, CB])
        rows3 = sb("rows3", [NP, CB, H])
        own_ps, hop_ps = ps("own_ps"), ps("hop_ps")
        turn_ps = [ps("turn_ps0"), ps("turn_ps1")]
        tab_ps = [ps("tab_ps0"), ps("tab_ps1")]
        x_in, picked, mixed, taken, chain = sem("x_in"), sem("picked"), sem("mixed"), sem("taken"), sem("chain")
        var_ready, root_ready, x1_ready, turned, copied = sem("var_ready"), sem("root_ready"), sem("x1_ready"), sem("turned"), sem("copied")
        tab_done, tab_ready, out = sem("tab_done"), sem("tab_ready"), sem("out")
        passed = sem("passed")
        block = ctx.enter_context(nc.Block())
        sums = mem["sums"][:, 0:N].rearrange("f (p b) -> f b p", b=NB)
        xr = mem["xr"][:].rearrange("p (b d) -> p b d", d=D)
        x_t_dram = io["x_t"].rearrange("f (b p) -> f b p", p=NP)
        table = io["table2"].rearrange("(p b) h -> p b h", b=NB)

        @block.sync
        def _(sp):
            def step(c, nb):
                wait_apart(sp, mixed, c, passed)
                sp.dma_start(x_t[:, 0:nb, :], x_t_dram[:, ds(c * CB, nb), :]).then_inc(x_in, 16)
                wait_apart(sp, tab_ready, c + 1, passed)
                sp.dma_start(table[:, ds(c * CB, nb), :], rows3[:, 0:nb, :]).then_inc(out, 16)

            over_chunks(sp, plan, step)
            sp.wait_ge(out, 16 * -(-NB // CB))

        @block.scalar
        def _(act):
            def step(c, nb):
                wait(act, mixed, c)
                act.copy(part[:, 0:nb, :], sums[:, ds(c * CB, nb), :]).then_inc(picked, 1)
                act.wait_ge(var_ready, c + 1)
                act.activation(stat[:, 4, 0:nb], stat[:, 3, 0:nb], ACT.Sqrt).then_inc(root_ready, 1)
                act.wait_ge(turned, c + 1)
                wait(act, tab_done, c)
                for q in range(-(-nb // 4)):
                    cp = act.copy(x1_t[:, q * 4:q * 4 + 4, :], turn_ps[q][0:D, 0:4 * NP].rearrange("f (b p) -> f b p", p=NP))
                cp.then_inc(copied, 1)

            over_chunks(act, plan, step)

        @block.tensor
        def _(pe):
            def step(c, nb):
                pe.wait_ge(x_in, c * 16 + 16)
                pe.wait_ge(picked, c + 1)
                wait(pe, taken, c)
                for b in range(nb):
                    pe.matmul(own_ps[0:NP, b * D:(b + 1) * D], x_t[:, b, :], mem["w0"][:], start=True, stop=True)
                    mm = pe.matmul(hop_ps[0:NP, b * D:(b + 1) * D], part[:, b, :], mem["w12"][:], start=True, stop=True)
                mm.then_inc(mixed, 1)
                wait(pe, copied, c)
                wait_apart(pe, x1_ready, c + 1, passed)
                for b in range(nb):
                    tr = pe.transpose(turn_ps[b // 4][0:D, b % 4 * NP:(b % 4 + 1) * NP], acc[:, b, :], mem["ident"][0:NP, 0:NP])
                tr.then_inc(turned, 1)
                pe.wait_ge(copied, c + 1)
                wait(pe, tab_ready, c)
                for b in range(nb):
                    mm = pe.matmul(tab_ps[b // 4][0:NP, b % 4 * H:(b % 4 + 1) * H], x1_t[:, b, :], mem["w1x"][:], start=True, stop=True)
                mm.then_inc(tab_done, 1)

            over_chunks(pe, plan, step)

        @block.vector
        def _(v):
            count = [0]
            steps = 16

            def step(c, nb):
                count[0] = 0

                def link(ins):
                    count[0] += 1
                    ins.then_inc(chain, 1)
                    v.wait_ge(chain, c * steps + count[0])

                at = ds(c * CB, nb)
                a, x = acc[:, 0:nb, :], xr[:, at, :]
                flat = lambda bank: bank[0:NP, 0:nb * D].rearrange("p (b d) -> p b d", d=D)
                v.wait_ge(mixed, c + 1)
                wait(v, turned, c)
                link(v.tensor_tensor(a, flat(hop_ps), mem["norm"][:, at].unsqueeze(2).broadcast_to([NP, nb, D]), ALU.mult))
                link(v.tensor_tensor(a, a, flat(own_ps), ALU.add))
                v.sem_inc(taken, 1)
                link(v.tensor_tensor(a, a, x, ALU.add))
                link(v.tensor_tensor(a, a, mem["bias0"][0:NP, :].unsqueeze(1).broadcast_to([NP, nb, D]), ALU.add))
                last = layernorm(v, link, mem, a, sq[:, 0:nb, :], stat, a, nb, D,
                                 lambda: v.wait_ge(root_ready, c + 1), lambda: v.sem_inc(var_ready, 1), NP)
                link(last)
                v.sem_inc(passed, 1)
                v.tensor_copy(x, a).then_inc(x1_ready, 1)
                assert count[0] == steps, count[0]
                v.wait_ge(tab_done, c + 1)
                wait(v, out, c * 16)
                for q in range(-(-nb // 4)):
                    add = v.tensor_tensor(rows3[:, q * 4:q * 4 + 4, :], tab_ps[q][0:NP, 0:4 * H].rearrange("p (b h) -> p b h", h=H),
                                          mem["b1"][0:NP, :].unsqueeze(1).broadcast_to([NP, 4, H]), ALU.add)
                add.then_inc(tab_ready, 1)

            over_chunks(v, plan, step)


def second_layer(nc, plan, mem, io):
    N, D, H, NB, NP, CB = plan.N, plan.D, plan.H, plan.NB, plan.NP, plan.CB
    with ExitStack() as ctx:
        sb = lambda n, s: ctx.enter_context(nc.sbuf_tensor("s_" + n, s, F32))
        ps = lambda n: ctx.enter_context(nc.psum_tensor("s_" + n, [P, 512], F32))
        sem = lambda n: ctx.enter_context(nc.semaphore("s_" + n))
        part = sb("part", [P, CB, NP])
        cat = sb("cat", [NP, CB, 2 * D])
        add2 = sb("add2", [NP, CB, D])
        cat_t = sb("cat_t", [2 * D, CB, NP])
        hid_t = sb("hid_t", [D, CB, NP])
        acc, sq = sb("acc", [NP, CB, D]), sb("sq", [NP, CB, D])
        stat = sb("stat", [NP, 7, CB])
        c3 = sb("c3", [D, 1])
        agg_ps, out_ps, c3_ps = ps("agg_ps"), ps("out_ps"), ps("c3_ps")
        turn_ps = [ps("turn_ps0"), ps("turn_ps1")]
        hid_ps = [ps("hid_ps0"), ps("hid_ps1")]
        picked, agg_done, cat_ready, turned, copied, hid_done = sem("picked"), sem("agg_done"), sem("cat_ready"), sem("turned"), sem("copied"), sem("hid_done")
        hid_ready, mlp_done, taken, chain, c3_done, c3_ready = sem("hid_ready"), sem("mlp_done"), sem("taken"), sem("chain"), sem("c3_done"), sem("c3_ready")
        var_ready, root_ready, done, out = sem("var_ready"), sem("root_ready"), sem("done"), sem("out")
        passed = sem("passed")
        block = ctx.enter_context(nc.Block())
        sums = mem["sums"][:, 0:N].rearrange("f (p b) -> f b p", b=NB)
        xr = mem["xr"][:].rearrange("p (b d) -> p b d", d=D)
        out_dram = io["out"].rearrange("(p b) d -> p b d", b=NB)

        @block.sync
        def _(sp):
            def step(c, nb):
                wait_apart(sp, done, c + 1, passed)
                sp.dma_start(out_dram[:, ds(c * CB, nb), :], acc[:, 0:nb, :]).then_inc(out, 16)

            over_chunks(sp, plan, step)
            sp.wait_ge(out, 16 * -(-NB // CB))

        @block.scalar
        def _(act):
            act.wait_ge(c3_ready, 1)

            def step(c, nb):
                wait(act, agg_done, c)
                act.copy(part[:, 0:nb, :], sums[:, ds(c * CB, nb), :]).then_inc(picked, 1)
                act.wait_ge(turned, c + 1)
                wait(act, hid_done, c)
                for q in range(-(-nb // 4)):
                    cp = act.copy(cat_t[:, q * 4:q * 4 + 4, :], turn_ps[q][:, 0:4 * NP].rearrange("f (b p) -> f b p", p=NP))
                cp.then_inc(copied, 1)
                act.wait_ge(hid_done, c + 1)
                wait(act, mlp_done, c)
                for q in range(-(-nb // 4)):
                    cp = act.activation(hid_t[:, q * 4:q * 4 + 4, :], hid_ps[q][0:D, 0:4 * NP].rearrange("f (b p) -> f b p", p=NP),
                                        ACT.Relu, bias=c3[:])
                cp.then_inc(hid_ready, 1)
                act.wait_ge(var_ready, c + 1)
                act.activation(stat[:, 4, 0:nb], stat[:, 3, 0:nb], ACT.Sqrt).then_inc(root_ready, 1)

            over_chunks(act, plan, step)

        @block.tensor
        def _(pe):
            pe.matmul(c3_ps[0:D, 0:1], mem["w3u"][:], mem["u0"][:], start=True, stop=True).then_inc(c3_done, 1)

            def step(c, nb):
                pe.wait_ge(picked, c + 1)
                wait(pe, cat_ready, c)
                for b in range(nb):
                    mm = pe.matmul(agg_ps[0:NP, b * D:(b + 1) * D], part[:, b, :], mem["w2"][:], start=True, stop=True)
                mm.then_inc(agg_done, 1)
                pe.wait_ge(cat_ready, c + 1)
                wait(pe, copied, c)
                for b in range(nb):
                    tr = pe.transpose(turn_ps[b // 4][:, b % 4 * NP:(b % 4 + 1) * NP], cat[:, b, :], mem["ident"][0:NP, 0:NP])
                tr.then_inc(turned, 1)
                pe.wait_ge(copied, c + 1)
                wait(pe, hid_ready, c)
                for q in range(-(-nb // 4)):
                    mm = pe.matmul(hid_ps[q][0:D, 0:4 * NP], mem["w3xa"][:], cat_t[:, q * 4:q * 4 + 4, :].rearrange("f b p -> f (b p)"),
                                   start=True, stop=True)
                mm.then_inc(hid_done, 1)
                pe.wait_ge(hid_ready, c + 1)
                wait(pe, taken, c)
                for b in range(nb):
                    mm = pe.matmul(out_ps[0:NP, b * D:(b + 1) * D], hid_t[:, b, :], mem["w4"][:], start=True, stop=True)
                mm.then_inc(mlp_done, 1)

            over_chunks(pe, plan, step)

        @block.vector
        def _(v):
            steps = 17
            v.wait_ge(c3_done, 1)
            v.tensor_tensor(c3[:], c3_ps[0:D, 0:1], mem["b3"][:], ALU.add).then_inc(c3_ready, 1)

            def step(c, nb):
                count = [0]

                def link(ins):
                    count[0] += 1
                    ins.then_inc(chain, 1)
                    v.wait_ge(chain, c * steps + count[0])

                at = ds(c * CB, nb)
                wide = lambda a: a.unsqueeze(2).broadcast_to([NP, nb, D])
                row = lambda a: a[0:NP, :].unsqueeze(1).broadcast_to([NP, nb, D])
                flat = lambda bank: bank[0:NP, 0:nb * D].rearrange("p (b d) -> p b d", d=D)
                a, x = acc[:, 0:nb, :], xr[:, at, :]
                v.wait_ge(agg_done, c + 1)
                wait(v, turned, c)
                v.sem_inc(passed, 1)
                link(v.tensor_copy(cat[:, 0:nb, 0:D], x))
                link(v.tensor_tensor(add2[:, 0:nb, :], row(mem["b2"]), wide(mem["some"][:, at]), ALU.mult))
                link(v.tensor_tensor(cat[:, 0:nb, D:2 * D], flat(agg_ps), wide(mem["inv"][:, at]), ALU.mult))
                v.tensor_tensor(cat[:, 0:nb, D:2 * D], cat[:, 0:nb, D:2 * D], add2[:, 0:nb, :], ALU.add).then_inc(cat_ready, 1)
                v.wait_ge(mlp_done, c + 1)
                wait(v, out, c * 16)
                link(v.tensor_tensor(a, flat(out_ps), x, ALU.add))
                v.sem_inc(taken, 1)
                link(v.tensor_tensor(a, a, row(mem["b4"]), ALU.add))
                last = layernorm(v, link, mem, a, sq[:, 0:nb, :], stat, a, nb, D,
                                 lambda: v.wait_ge(root_ready, c + 1), lambda: v.sem_inc(var_ready, 1), NP)
                last.then_inc(done, 1)
                v.sem_inc(chain, steps - count[0])

            over_chunks(v, plan, step)


def build(nc, plan, io):
    N, D, NB, NP, T, G, H = plan.N, plan.D, plan.NB, plan.NP, plan.T, plan.G, plan.H
    with ExitStack() as ctx:
        mem = {}
        for name, shape, dt in (
            ("xr", [NP, NB * D], F32),
            ("sums", [P, N + plan.WIN], F32),
            ("stage", [NP, NB * D], F32),
            ("rel0", [P, T], F32),
            ("base_row0", [1, G], I32),
            ("passes", [1, 1], I32),
            ("iota_f", [P, P], F32),
            ("norm", [NP, NB], F32), ("norm2", [NP, NB], F32),
            ("inv", [NP, NB], F32), ("some", [NP, NB], F32),
            ("ident", [P, P], F32),
            ("w0", [D, D], F32), ("w12", [2 * D, D], F32), ("bias0", [P, D], F32),
            ("w1x", [D, H], F32), ("w1e", [plan.FE, H], F32), ("b1", [P, H], F32),
            ("w2", [H, D], F32), ("b2", [P, D], F32),
            ("w3xa", [2 * D, D], F32), ("w3u", [D, D], F32), ("b3", [D, 1], F32),
            ("w4", [D, D], F32), ("b4", [P, D], F32), ("u0", [D, 1], F32),
        ):
            mem[name] = ctx.enter_context(nc.sbuf_tensor("m_" + name, shape, dt))
        prologue(nc, plan, mem, io)
        edge_sums(nc, plan, mem, io, "h1_", io["table0"], 0)
        second_table(nc, plan, mem, io)
        edge_sums(nc, plan, mem, io, "h2_", io["table1"], D)
        first_layer(nc, plan, mem, io)
        edge_sums(nc, plan, mem, io, "e_", io["table2"], 0, edge_mlp=True)
        second_layer(nc, plan, mem, io)


def kernel(**inputs):
    import numpy as np
    import concourse.bacc as bacc
    from concourse.bass_utils import run_bass_kernel_spmd

    x, src, dst, edge = (np.asarray(inputs[k]) for k in ("x", "src", "dst", "edge_attr_32"))
    w, b0, u, w3 = (np.asarray(inputs[k]) for k in ("L0_gnn_weight", "L0_gnn_bias", "L1_gnn_u", "L1_gnn_W3"))
    w1, b1, w2, b2, b3, w4, b4 = (np.asarray(inputs["L1_gnn_" + k]) for k in ("W1", "b1", "W2", "b2", "b3", "W4", "b4"))
    N, D = x.shape
    E, FE = edge.shape
    plan = Plan(N, E, D, FE, w1.shape[1])
    NB, NP, T, TH = plan.NB, plan.NP, plan.T, plan.TH
    pad = T * P - E
    src_p = np.concatenate([src, np.zeros(pad, src.dtype)])
    dst_p = np.concatenate([dst, np.full(pad, N, dst.dtype)])
    edge_p = np.concatenate([edge, np.zeros((pad, FE), edge.dtype)])
    rows = lambda a: np.ascontiguousarray(np.broadcast_to(a, (P, a.shape[0])))
    arrays = {
        "x": x,
        "x_t": x.reshape(NP, NB, D).transpose(2, 1, 0).reshape(D, N),
        "src": src_p.reshape(T // TH, TH, P).transpose(0, 2, 1),
        "dst": dst_p.reshape(T, P).T,
        "edge_t": edge_p.reshape(T // TH, TH * P, FE).transpose(0, 2, 1),
        "ident": np.eye(P, dtype=x.dtype),
        "w0": w[:, 0:D].T, "w12": w[:, D:3 * D].T, "bias0": rows(b0),
        "w1x": w1[0:D], "w1e": w1[D:D + FE], "b1": rows(b1),
        "w2": w2, "b2": rows(b2),
        "w3xa": w3[0:2 * D], "w3u": w3[2 * D:3 * D], "b3": b3[:, None],
        "w4": w4, "b4": rows(b4), "u0": u[0][:, None],
    }
    arrays = {"in_" + k: np.ascontiguousarray(a) for k, a in arrays.items()}
    nc = bacc.Bacc("TRN2", target_bir_lowering=False, num_devices=1)
    io = {k[3:]: nc.dram_tensor(k, a.shape, mybir.dt.from_np(a.dtype), kind="ExternalInput").ap() for k, a in arrays.items()}
    io["out"] = nc.dram_tensor("out_0", (N, D), F32, kind="ExternalOutput").ap()
    for name, shape, dt in (("table0", (N, D), F32), ("table1", (N, D), F32), ("table2", (N, plan.H), F32), ("scratch_base", (plan.G,), I32)):
        io[name] = nc.dram_tensor(name, shape, dt, kind="Internal").ap()
    build(nc, plan, io)
    r = run_bass_kernel_spmd(nc, [arrays], core_ids=[0])
    return r.results[0]["out_0"]
```

```python
from contextlib import ExitStack

import concourse.bass as bass
from concourse import mybir

ALU = mybir.AluOpType
ACT = mybir.ActivationFunctionType
AX = mybir.AxisListType
F32 = mybir.dt.float32
BF16 = mybir.dt.bfloat16
I32 = mybir.dt.int32

P = 128
EPS = 1e-5


class Plan:

    def __init__(self, nodes, edges, feat, edge_feat, hidden):
        self.N, self.E, self.D, self.FE, self.H = nodes, edges, feat, edge_feat, hidden
        self.NB = 100
        self.NP = nodes // self.NB
        assert self.NP * self.NB == nodes and self.NP <= P
        self.TG = 4
        self.GB = 8
        self.TH = self.TG * self.GB // 2
        per_turn = P * self.TG * self.GB
        self.TURNS = -(-edges // per_turn)
        self.T = self.TURNS * self.TG * self.GB
        self.G = self.TURNS * self.GB
        self.WIN = 128
        self.HT = 6
        self.HN = 208
        self.HW = 12
        self.CB = 4
        self.CHUNKS = self.NB // self.CB
        self.slices = [(a, a + 25) for a in range(0, self.NB, 25)]


def ds(start, size):
    return bass.ds(start, size)


def wait(engine, semaphore, value):
    if not isinstance(value, int) or value > 0:
        engine.wait_ge(semaphore, value)


def wait_apart(engine, semaphore, value, passed):
    if not isinstance(value, int):
        engine.wait_ge(semaphore, value)
        engine.sem_inc(passed, 1)
    elif value > 0:
        engine.wait_ge(semaphore, value)


def prologue(nc, plan, mem, io):
    N, D, NB, NP, T, G, TG = plan.N, plan.D, plan.NB, plan.NP, plan.T, plan.G, plan.TG
    U = 16
    HT = plan.HT * plan.TG * plan.GB
    HB = 2
    GC = G // 4
    with ExitStack() as ctx:
        sb = lambda n, s, d: ctx.enter_context(nc.sbuf_tensor(n, s, d))
        ps = lambda n, s, d: ctx.enter_context(nc.psum_tensor(n, s, d))
        sem = lambda n: ctx.enter_context(nc.semaphore(n))
        dst_i = sb("dst_i", [P, T], I32)
        dst_f = sb("dst_f", [P, T], F32)
        hi_i = sb("hi_i", [P, T], I32)
        digit_hi = sb("digit_hi", [P, HT], F32)
        digit_hi2 = sb("digit_hi2", [P, T], F32)
        digit_lo = sb("digit_lo", [P, T], F32)
        fix = sb("fix", [P, T], F32)
        hi_b = sb("hi_b", [P, T], BF16)
        lo_b = sb("lo_b", [P, T], BF16)
        iota_i = sb("iota_i", [P, P], I32)
        iota_head = mem["sums"][:, NB * D:NB * (D + plan.HW)].bitcast(I32)
        iota_b = sb("iota_b", [P, NP, U], BF16)
        one_hi = sb("one_hi", [P, HB, NP, U], BF16)
        one_lo = sb("one_lo", [P, HB, NB, U], BF16)
        stage = mem["sums"][0:NP, 0:NB * D].rearrange("p (b d) -> p b d", d=D)
        deg = sb("deg", [NP, NB], F32)
        tmp = sb("tmp", [NP, NB], F32)
        tmp2 = sb("tmp2", [NP, NB], F32)
        least = sb("least", [P, G], F32)
        least_t = sb("least_t", [GC, 4], F32)
        least_i = sb("least_i", [GC, 4], I32)
        base_bc = sb("base_bc", [P, G], F32)
        base_bi = sb("base_bi", [P, G], I32)
        far = sb("far", [P, 3], F32)
        far_i = sb("far_i", [1, 1], I32)
        head_src = sb("head_src", [P, plan.HT * 2, plan.TH], I32)
        deg_ps = ps("deg_ps", [NP, 512], F32)
        tr_ps = ps("tr_ps", [P, 512], F32)

        loaded = sem("p_loaded")
        iota_ready = sem("p_iota")
        dve = sem("p_dve")
        hot_ready = sem("p_hot_ready")
        hot_used = sem("p_hot_used")
        turned = sem("p_turned")
        scaled = sem("p_sqrt")
        spread = sem("p_spread")
        table_out = sem("p_table_out")
        table_ready = sem("p_table_ready")
        x_loaded = sem("p_x_loaded")
        w_loaded = sem("p_w_loaded")
        head_loaded = sem("p_head_loaded")
        counts_clear = sem("p_counts_clear")
        marks = {}

        block = ctx.enter_context(nc.Block())

        @block.vector
        def _(v):
            count = [0]

            def link(ins, mark=None):
                count[0] += 1
                ins.then_inc(dve, 1)
                v.wait_ge(dve, count[0])
                if mark:
                    marks[mark] = count[0]

            def digits(a, n, hi, lo):
                q, h, l, f = hi_i[:, 0:n], digit_hi2[:, 0:n], digit_lo[:, 0:n], fix[:, 0:n]
                link(v.tensor_scalar(l, a, 1.0 / NB, 0.5 / NB - 0.5, ALU.mult, ALU.add))
                link(v.tensor_copy(q, l))
                link(v.tensor_copy(h, q))
                link(v.scalar_tensor_tensor(out=l, in0=h, scalar=-float(NB), in1=a, op0=ALU.mult, op1=ALU.add))
                link(v.tensor_scalar(f, l, float(NB), None, ALU.is_ge))
                link(v.tensor_tensor(hi, h, f, ALU.add))
                link(v.scalar_tensor_tensor(out=lo, in0=f, scalar=-float(NB), in1=l, op0=ALU.mult, op1=ALU.add))

            v.wait_ge(iota_ready, 2)
            link(v.tensor_copy(mem["iota_2"][:], iota_head))
            link(v.tensor_copy(iota_b[:], iota_i[:, 0:NP].unsqueeze(2).broadcast_to([P, NP, U])))
            link(v.tensor_copy(mem["iota_f"][:], iota_i[:]))
            v.wait_ge(loaded, 16)
            link(v.tensor_copy(dst_f[:], dst_i[:]))
            digits(dst_f[:], T, hi_b[:], lo_b[:])

            def hot(n, k):
                wait(v, hot_used, n - HB + 1)
                tiles = lambda a, w: a[:, ds(n * U, U)].unsqueeze(1).broadcast_to([P, w, U])
                v.tensor_tensor(one_hi[:, k], tiles(hi_b, NP), iota_b[:], ALU.is_equal)
                v.tensor_tensor(one_lo[:, k], tiles(lo_b, NB), iota_b[:, 0:NB], ALU.is_equal).then_inc(hot_ready, 1)

            for k in range(HB):
                hot(k, k)
            with v.Fori(1, T // U // HB) as i:
                for k in range(HB):
                    hot(i * HB + k, k)
            link(v.tensor_reduce(least[:], dst_f[:].rearrange("p (g t) -> p g t", t=TG), AX.X, ALU.min), "least")

            v.wait_ge(hot_used, T // U)
            link(v.tensor_copy(deg[:], deg_ps[:, 0:NB]))
            link(v.tensor_scalar(tmp[:], deg[:], 1.0, None, ALU.max), "deg_max")
            link(v.reciprocal(mem["inv"][:], tmp[:]))
            link(v.tensor_tensor(mem["some"][:], deg[:], mem["inv"][:], ALU.mult))
            v.wait_ge(scaled, 1)
            link(v.reciprocal(mem["norm"][:], tmp2[:]))
            link(v.tensor_tensor(tmp2[:], mem["norm"][:], mem["norm"][:], ALU.mult))
            link(v.tensor_tensor(tmp2[:], tmp2[:], tmp[:], ALU.mult))
            link(v.tensor_scalar(tmp2[:], tmp2[:], -0.5, 1.5, ALU.mult, ALU.add))
            link(v.tensor_tensor(mem["norm"][:], tmp2[:], mem["norm"][:], ALU.mult))
            link(v.tensor_tensor(mem["norm2"][:], mem["norm"][:], mem["norm"][:], ALU.mult))
            v.wait_ge(x_loaded, 16)
            for a, b in plan.slices:
                v.tensor_tensor(stage[:, a:b, :], mem["xr"][:].rearrange("p (b d) -> p b d", d=D)[:, a:b, :],
                                mem["norm"][:, a:b].unsqueeze(2).broadcast_to([NP, b - a, D]), ALU.mult).then_inc(table_ready, 1)

            v.wait_ge(turned, 1)
            link(v.tensor_reduce(least_t[:], tr_ps[0:GC, :].rearrange("q (c p) -> q c p", p=P), AX.X, ALU.min))
            link(v.tensor_copy(least_i[:], least_t[:]), "least_i")
            v.wait_ge(spread, 48)
            link(v.tensor_copy(base_bc[:], base_bi[:]))
            link(v.tensor_tensor(mem["rel"][:].rearrange("p (g t) -> p g t", t=TG), dst_f[:].rearrange("p (g t) -> p g t", t=TG),
                                 base_bc[:].unsqueeze(2).broadcast_to([P, G, TG]), ALU.subtract))
            link(v.tensor_reduce(far[:, 0:1], mem["rel"][:], AX.X, ALU.max))
            link(v.tensor_reduce(far[:, 1:2], mem["rel"][:, 0:HT], AX.X, ALU.max))
            link(v.tensor_reduce(far[:, 2:3], dst_f[:, 0:HT], AX.X, ALU.max), "far")
            link(v.tensor_scalar(mem["base_head"][:], mem["base_row0"][:, 0:HT // TG], plan.HN, None, ALU.min))
            v.wait_ge(head_loaded, 16)
            link(v.tensor_copy(digit_hi[:, 0:HT], head_src[:].rearrange("p h t -> p (h t)")))
            digits(digit_hi[:, 0:HT], HT, mem["head_p"][:], mem["head_b"][:])
            link(v.tensor_scalar(fix[:, 0:HT], mem["rel"][:, 0:HT], float(plan.HW), float(NB * plan.HW), ALU.is_ge, ALU.mult))
            link(v.tensor_tensor(fix[:, 0:HT], fix[:, 0:HT], mem["rel"][:, 0:HT], ALU.add))
            link(v.scalar_tensor_tensor(out=mem["head_b"][:], in0=mem["head_b"][:], scalar=float(plan.HW), in1=fix[:, 0:HT], op0=ALU.mult, op1=ALU.add))
            v.wait_ge(turned, 2)
            link(v.tensor_reduce(mem["extremes"][:], tr_ps[0:1, 0:3 * P].rearrange("a (k p) -> a k p", p=P), AX.X, ALU.max))
            link(v.tensor_copy(far_i[:], mem["extremes"][:, 0:1]))
            link(v.tensor_scalar(far_i[:], far_i[:], 7, None, ALU.arith_shift_right))
            link(v.tensor_scalar(mem["passes_any"][:], far_i[:], 1, None, ALU.add))
            for k, limit in enumerate((plan.WIN, plan.HW, plan.HN, 256)):
                link(v.memset(mem["limits"][:, k:k + 1], float(limit)))

        @block.sync
        def _(sp):
            sp.dma_start(dst_i[:], io["dst"]).then_inc(loaded, 16)
            sp.dma_start(head_src[:], io["src"][0:plan.HT * 2].rearrange("h p t -> p h t")).then_inc(head_loaded, 16)
            sp.dma_start(mem["xr"][:], io["x"].rearrange("(p b) d -> p (b d)", b=NB)).then_inc(x_loaded, 16)
            for name in ("ident", "w0", "w12", "bias0", "w1x", "w1e", "w2", "b2", "w3xa", "w3u", "b3", "w4", "u0"):
                sp.dma_start(mem[name][:], io[name]).then_inc(w_loaded, 16)
            for k, (a, b) in enumerate(plan.slices):
                sp.wait_ge(table_ready, k + 1)
                sp.dma_start(io["table0"].rearrange("(p b) d -> p b d", b=NB)[:, a:b, :], stage[:, a:b, :]).then_inc(table_out, 16)
            sp.wait_ge(dve, marks["least_i"])
            sp.dma_start(io["scratch_base"].rearrange("(q c) -> q c", c=4), least_i[:]).then_inc(spread, 16)
            sp.wait_ge(spread, 16)
            sp.dma_start(mem["base_row0"][:], io["scratch_base"].rearrange("(a g) -> a g", a=1)).then_inc(spread, 16)
            sp.dma_start(base_bi[:], io["scratch_base"].rearrange("(a g) -> a g", a=1).broadcast_to([P, G])).then_inc(spread, 16)
            sp.wait_ge(table_out, 16 * len(plan.slices))
            sp.wait_ge(w_loaded, 16 * 13)
            sp.wait_ge(spread, 48)

        @block.gpsimd
        def _(pool):
            pool.iota(iota_i[:], [[1, P]], base=0, channel_multiplier=0).then_inc(iota_ready, 1)
            pool.iota(iota_head, [[1, NB * plan.HW]], base=0, channel_multiplier=0).then_inc(iota_ready, 1)
            pool.memset(mem["counts"][:], 0.0).then_inc(counts_clear, 1)
            pool.wait_ge(counts_clear, 1)

        @block.scalar
        def _(act):
            act.wait_ge(dve, marks["deg_max"])
            act.activation(tmp2[:], tmp[:], ACT.Sqrt).then_inc(scaled, 1)

        @block.tensor
        def _(pe):
            def turn(n, k, start, stop):
                pe.wait_ge(hot_ready, n + 1)
                for u in range(U):
                    mm = pe.matmul(deg_ps[:, 0:NB], one_hi[:, k, :, u], one_lo[:, k, :, u],
                                   start=start and u == 0, stop=stop and u == U - 1)
                mm.then_inc(hot_used, 1)

            n_hot = T // U
            for k in range(HB):
                turn(k, k, k == 0, False)
            with pe.Fori(1, n_hot // HB - 1) as i:
                for k in range(HB):
                    turn(i * HB + k, k, False, False)
            for k in range(HB):
                turn(n_hot - HB + k, k, False, k == HB - 1)
            pe.wait_ge(w_loaded, 16 * 13)
            pe.wait_ge(dve, marks["least"])
            for c in range(4):
                tr = pe.transpose(tr_ps[0:GC, c * P:(c + 1) * P], least[:].rearrange("p (q c) -> p c q", c=4)[:, c, :], mem["ident"][:])
            tr.then_inc(turned, 1)
            pe.wait_ge(dve, marks["far"])
            for k in range(3):
                tr = pe.transpose(tr_ps[0:1, k * P:(k + 1) * P], far[:, k:k + 1], mem["ident"][:])
            tr.then_inc(turned, 1)


class Side:

    def __init__(self, ctx, nc, plan, mem, io, tag, low, table):
        self.plan, self.mem, self.io, self.low, self.table = plan, mem, io, low, table
        name = tag + type(self).__name__ + "_"
        sb = lambda n, s, d=F32: ctx.enter_context(nc.sbuf_tensor(name + n, s, d))
        sem = lambda n: ctx.enter_context(nc.semaphore(name + n))
        self.place(sb, lambda n: ctx.enter_context(nc.psum_tensor(name + n, [P, 512], F32)), sem)

    def place(self, sb, ps, sem):
        pass

    def blocks(self, name, c):
        p = self.plan
        return self.mem[name][:].rearrange("p (b d) -> p b d", d=p.D)[:, ds(c * p.CB, p.CB), :]

    def row(self, a):
        p = self.plan
        return a[0:p.NP, :].unsqueeze(1).broadcast_to([p.NP, p.CB, p.D])

    def wide(self, name, c):
        p = self.plan
        return self.mem[name][:, ds(c * p.CB, p.CB)].unsqueeze(2).broadcast_to([p.NP, p.CB, p.D])

    def flat(self, bank):
        p = self.plan
        return bank[0:p.NP, 0:p.CB * p.D].rearrange("p (b d) -> p b d", d=p.D)

    def sync(self, sp, c, half):
        pass

    def scalar(self, act, c, half):
        pass

    def tensor(self, pe, c, half):
        pass

    def vector(self, v, c, half):
        pass


class OwnPart(Side):

    def place(self, sb, ps, sem):
        p = self.plan
        self.x_t = sb("x_t", [p.D, p.CB, p.NP])
        self.own_ps = ps("own_ps")
        self.x_in, self.mixed, self.added, self.done, self.passed = (sem(n) for n in ("x_in", "mixed", "added", "done", "passed"))

    def sync(self, sp, c, half):
        if half == 0:
            wait_apart(sp, self.mixed, c, self.passed)
            chunk = self.io["x_t"].rearrange("f (b p) -> f b p", p=self.plan.NP)[:, ds(c * self.plan.CB, self.plan.CB), :]
            sp.dma_start(self.x_t[:], chunk).then_inc(self.x_in, 16)

    def tensor(self, pe, c, half):
        D, NP = self.plan.D, self.plan.NP
        if half == 0:
            wait(pe, self.added, c)
            pe.wait_ge(self.x_in, c * 16 + 16)
            for b in range(self.plan.CB):
                mm = pe.matmul(self.own_ps[0:NP, b * D:(b + 1) * D], self.x_t[:, b, :], self.mem["w0"][:], start=True, stop=True)
            mm.then_inc(self.mixed, 1)

    def vector(self, v, c, half):
        x = self.blocks("xr", c)
        if half == 1:
            v.wait_ge(self.mixed, c + 1)
            v.tensor_tensor(x, x, self.flat(self.own_ps), ALU.add).then_inc(self.added, 1)
            v.wait_ge(self.added, c + 1)
            v.tensor_tensor(x, x, self.row(self.mem["bias0"]), ALU.add).then_inc(self.done, 1)


class FirstHopPart(Side):

    def place(self, sb, ps, sem):
        p = self.plan
        self.part = sb("part", [p.D, p.CB, p.NP])
        self.scaled_part = sb("scaled_part", [p.NP, p.CB, p.D])
        self.hop_ps = ps("hop_ps")
        self.picked, self.mixed, self.scaled, self.done = (sem(n) for n in ("picked", "mixed", "scaled", "done"))

    def scalar(self, act, c, half):
        p = self.plan
        if half == 0:
            wait(act, self.mixed, c)
            act.copy(self.part[:], self.mem["sums"][0:p.D, 0:p.N].rearrange("f (p b) -> f b p", b=p.NB)[:, ds(c * p.CB, p.CB), :]).then_inc(self.picked, 1)

    def tensor(self, pe, c, half):
        D, NP = self.plan.D, self.plan.NP
        if half == 0:
            wait(pe, self.scaled, c)
            pe.wait_ge(self.picked, c + 1)
            for b in range(self.plan.CB):
                mm = pe.matmul(self.hop_ps[0:NP, b * D:(b + 1) * D], self.part[:, b, :], self.mem["w12"][0:D], start=True, stop=True)
            mm.then_inc(self.mixed, 1)

    def vector(self, v, c, half):
        x = self.blocks("xr", c)
        if half == 1:
            v.wait_ge(self.mixed, c + 1)
            wait(v, self.done, c)
            v.tensor_tensor(self.scaled_part[:], self.flat(self.hop_ps), self.wide("norm", c), ALU.mult).then_inc(self.scaled, 1)
            v.wait_ge(self.scaled, c + 1)
            v.tensor_tensor(x, x, self.scaled_part[:], ALU.add).then_inc(self.done, 1)


class MeanBias(Side):

    def place(self, sb, ps, sem):
        self.done = sem("done")

    def vector(self, v, c, half):
        if half == 0:
            v.tensor_tensor(self.blocks("add2", c), self.row(self.mem["b2"]), self.wide("some", c), ALU.mult).then_inc(self.done, 1)


class TableParts(Side):

    def place(self, sb, ps, sem):
        p = self.plan
        self.t = sb("t", [p.NP, p.CB, p.D])
        self.rest = sb("rest", [p.NP, p.CB, p.D])
        self.loaded, self.steps, self.passed = sem("loaded"), sem("steps"), sem("passed")

    def sync(self, sp, c, half):
        if half == 0:
            wait_apart(sp, self.steps, c * 5, self.passed)
            chunk = self.table.rearrange("(p b) d -> p b d", b=self.plan.NB)[:, ds(c * self.plan.CB, self.plan.CB), :]
            sp.dma_start(self.t[:], chunk).then_inc(self.loaded, 16)

    def vector(self, v, c, half):
        if half == 1:
            p = self.plan
            part = lambda s: self.mem["parts"][:, ds(c * p.CB, p.CB), s, :]
            v.wait_ge(self.loaded, c * 16 + 16)
            for k, (out, a, b) in enumerate(((part(0), self.t, None), (self.rest, self.t, part(0)), (part(1), self.rest, None),
                                             (self.t, self.rest, part(1)), (part(2), self.t, None))):
                out = out[:] if out in (self.rest, self.t) else out
                ins = v.tensor_copy(out, a[:]) if b is None else v.tensor_tensor(out, a[:], b, ALU.subtract)
                ins.then_inc(self.steps, 1)
                v.wait_ge(self.steps, c * 5 + k + 1)


class HeadCounts(Side):

    def place(self, sb, ps, sem):
        p = self.plan
        self.hot_b = sb("hot_b", [P, p.TG, p.NB * p.HW], BF16)
        self.hot_p = sb("hot_p", [P, p.TG, p.NP], BF16)
        self.hot_ready, self.hot_used, self.added = sem("hot_ready"), sem("hot_used"), sem("added")

    def units(self, c):
        first = isinstance(c, int) and c == 0
        return lambda half: None if first else (c - 1) * 2 + half

    def tensor(self, pe, c, half):
        p, u = self.plan, self.units(c)(half)
        if u is None:
            return
        wait(pe, self.added, u)
        for t in range(p.TG):
            pe.wait_ge(self.hot_ready, u * p.TG + t + 1)
            for k in range(4):
                cols = p.NB // 4 * p.HW
                mm = pe.matmul(self.mem["banks"][0:p.NP, k, 0:cols], self.hot_p[:, t, :], self.hot_b[:, t, k * cols:(k + 1) * cols],
                               start=(t == 0), stop=(t == p.TG - 1))
            mm.then_inc(self.hot_used, 1)

    def vector(self, v, c, half):
        p, u = self.plan, self.units(c)(half)
        if u is None:
            return
        if not (isinstance(c, int) and c == 1 and half == 0):
            self.add(v, u - 1)
        for t in range(p.TG):
            wait(v, self.hot_used, (u - 1) * p.TG + t + 1)
            at = ds(u * p.TG + t, 1)
            v.tensor_scalar(self.hot_p[:, t, :], self.mem["iota_2"][:, 0:p.NP], self.mem["head_p"][:, at], None, ALU.is_equal)
            v.tensor_scalar(self.hot_b[:, t, :], self.mem["iota_2"][:], self.mem["head_b"][:, at], None, ALU.is_equal).then_inc(self.hot_ready, 1)

    def add(self, v, u):
        p = self.plan
        first = v.value_load(self.mem["base_head"][0:1, ds(u, 1)], min_val=0, max_val=p.HN)
        v.wait_ge(self.hot_used, (u + 1) * p.TG)
        wait(v, self.added, u)
        window = self.mem["counts"][:, :, ds(first, p.HW)].rearrange("p (k b) w -> p k b w", k=4)
        v.tensor_tensor(window, window, self.mem["banks"][0:p.NP, :, 0:p.NB // 4 * p.HW].rearrange("p k (b w) -> p k b w", w=p.HW),
                        ALU.add).then_inc(self.added, 1)


class HeadSums:

    def __init__(self, ctx, nc, plan, mem, io, tag, low, sides):
        self.plan, self.mem, self.io, self.low = plan, mem, io, low
        sem = lambda n: ctx.enter_context(nc.semaphore(tag + "head_" + n))
        self.tall = ctx.enter_context(nc.sbuf_tensor(tag + "head_tall", [plan.HN // 2, 2, 2 * plan.D], F32))
        self.multiplied, self.steps, self.turned, self.added = sem("multiplied"), sem("steps"), sem("turned"), sem("added")
        self.parts = next(s for s in sides if isinstance(s, TableParts))
        self.counter = next((s for s in sides if isinstance(s, HeadCounts)), None)
        if self.counter:
            self.most = ctx.enter_context(nc.sbuf_tensor(tag + "head_most", [plan.NP, 2], F32))
            self.flags = ctx.enter_context(nc.sbuf_tensor(tag + "head_flags", [1, 8], F32))
            self.whole, self.most_ready, self.most_turned, self.flag_steps = sem("whole"), sem("most_ready"), sem("most_turned"), sem("flag_steps")

    def multiply(self, pe):
        p, m = self.plan, self.mem
        half, W = p.HN // 2, 3 * p.D
        pe.wait_ge(self.parts.steps, 5 * p.CHUNKS)
        if self.counter:
            pe.wait_ge(self.whole, 1)

        def block(b, start, stop):
            for k in range(2):
                mm = pe.matmul(m["banks"][0:half, k, 0:W], m["counts"][:, ds(b, 1), k * half:(k + 1) * half].rearrange("p a n -> p (a n)"),
                               m["parts"][:, ds(b, 1)].rearrange("p a s d -> p (a s d)"), start=start, stop=stop)
            return mm

        for b in range(4):
            block(b, b == 0, False)
        with pe.Fori(1, p.NB // 4 - 1) as j:
            for k in range(4):
                block(j * 4 + k, False, False)
        for b in range(p.NB - 4, p.NB):
            mm = block(b, False, b == p.NB - 1)
        mm.then_inc(self.multiplied, 1)

    def add_parts(self, v):
        p, m = self.plan, self.mem
        D = p.D
        v.memset(self.tall[:], 0.0).then_inc(self.steps, 1)
        v.wait_ge(self.multiplied, 1)
        v.wait_ge(self.steps, 1)
        tall = self.tall[:, :, self.low:self.low + D]
        part = lambda s: m["banks"][0:p.HN // 2, 0:2, s * D:(s + 1) * D]
        v.tensor_copy(tall, part(2)).then_inc(self.steps, 1)
        v.wait_ge(self.steps, 2)
        v.tensor_tensor(tall, tall, part(1), ALU.add).then_inc(self.steps, 1)
        v.wait_ge(self.steps, 3)
        v.tensor_tensor(tall, tall, part(0), ALU.add).then_inc(self.steps, 1)

    def turn(self, pe):
        p = self.plan
        half = p.HN // 2
        pe.wait_ge(self.steps, 4)
        for k in range(2):
            tr = pe.transpose(self.mem["banks"][:, 2, k * half:(k + 1) * half], self.tall[:, k, :], self.mem["ident"][0:half, 0:half])
        tr.then_inc(self.turned, 1)
        if self.counter:
            pe.wait_ge(self.most_ready, 1)
            for k in range(2):
                tr = pe.transpose(self.mem["banks"][0:1, 3, k * P:k * P + p.NP], self.most[:, k:k + 1], self.mem["ident"][0:p.NP, 0:p.NP])
            tr.then_inc(self.most_turned, 1)

    def finish(self, v, sums_added):
        p = self.plan
        v.wait_ge(self.turned, 1)
        sums_added()
        at = self.mem["sums"][self.low:self.low + p.D, 0:p.HN]
        v.tensor_tensor(at, at, self.mem["banks"][self.low:self.low + p.D, 2, 0:p.HN], ALU.add).then_inc(self.added, 1)
        v.wait_ge(self.added, 1)

    def largest(self, v, k):
        p = self.plan
        h = p.NB // 2
        v.tensor_reduce(self.most[:, k:k + 1], self.mem["counts"][:, k * h:(k + 1) * h, :], AX.XY, ALU.max).then_inc(self.most_ready if k else self.flag_steps, 1)

    def decide(self, v):
        p, f = self.plan, self.flags
        steps = [1]

        def link(ins):
            steps[0] += 1
            ins.then_inc(self.flag_steps, 1)
            v.wait_ge(self.flag_steps, steps[0])

        v.wait_ge(self.flag_steps, 1)
        v.wait_ge(self.most_turned, 1)
        link(v.tensor_reduce(f[:, 3:4], self.mem["banks"][0:1, 3, 0:2 * P].rearrange("a (k q) -> a k q", q=P)[:, :, 0:p.NP], AX.XY, ALU.max))
        link(v.tensor_tensor(f[:, 4:7], self.mem["extremes"][:], self.mem["limits"][:, 0:3], ALU.is_ge))
        link(v.tensor_tensor(f[:, 7:8], f[:, 3:4], self.mem["limits"][:, 3:4], ALU.is_ge))
        link(v.tensor_reduce(f[:, 0:1], f[:, 4:8], AX.X, ALU.max))
        link(v.tensor_copy(f[:, 1:2], self.mem["passes_any"][:]))
        link(v.tensor_tensor(f[:, 2:3], f[:, 0:1], f[:, 1:2], ALU.mult))
        link(v.tensor_copy(self.mem["passes"][:], f[:, 2:3]))


def edge_sums(nc, plan, mem, io, tag, table, low, side_kinds, edge_mlp=False):
    N, D, T, G, TG, GB, TH, WIN, TURNS = plan.N, plan.D, plan.T, plan.G, plan.TG, plan.GB, plan.TH, plan.WIN, plan.TURNS
    F = plan.H if edge_mlp else D
    HG = GB // 2
    skip = 0 if edge_mlp else plan.HT
    with ExitStack() as ctx:
        sb = lambda n, s, d: ctx.enter_context(nc.sbuf_tensor(tag + n, s, d))
        ps = lambda n, s, d: ctx.enter_context(nc.psum_tensor(tag + n, s, d))
        sem = lambda n: ctx.enter_context(nc.semaphore(tag + n))
        index = sb("index", [P, 2, TH], I32)
        rows = sb("rows", [P, GB, TG, F], F32)
        hot = sb("hot", [P, 4, TG, WIN], F32)
        base = sb("base", [1, G], I32)
        seg_ps = [ps(f"seg_ps{k}", [P, 512], F32) for k in range(2)]
        if edge_mlp:
            edges = sb("edges", [plan.FE, 2, TH * P], F32)
            pre = sb("pre", [P, 2, TG, F], F32)
            hid = sb("hid", [P, 2, TG, F], F32)
            emb_ps = [ps(f"emb_ps{k}", [P, 512], F32) for k in range(2)]

        rows_in = [sem(f"rows_in{k}") for k in range(GB)]
        index_in = [sem(f"index_in{h}") for h in range(2)]
        hot_ready = sem("hot_ready")
        seg_done = sem("seg_done")
        sum_done = sem("sum_done")
        if edge_mlp:
            edges_in = [sem(f"edges_in{h}") for h in range(2)]
            emb_done = sem("emb_done")
            pre_ready = sem("pre_ready")
            hid_ready = sem("hid_ready")
        start = sem("start")
        decided = sem("decided")
        pass_done = sem("pass_done")
        pass_open = sem("pass_open")
        moved = sem("moved")
        passed = sem("passed")

        sides = [kind(ctx, nc, plan, mem, io, tag, low, table) for kind in side_kinds]
        head = None if edge_mlp else HeadSums(ctx, nc, plan, mem, io, tag, low, sides)
        block = ctx.enter_context(nc.Block())

        def passes(engine, turn, beside, last=None, between=None, reset=None, undo=None):
            between = between or (lambda k: None)

            def main_turn(m):
                turn(m + skip, m, m, lambda half: [beside(side, m, half) for side in sides])

            main_turn(0)
            main_turn(1)
            with engine.Fori(2, plan.CHUNKS) as m:
                main_turn(m)
            main = TURNS - skip
            marks = [plan.CHUNKS + 3 * k for k in range(5)] if head else [plan.CHUNKS]
            for k, (a, b) in enumerate(zip(marks, [*marks[1:], main])):
                between(k)
                with engine.Fori(a, b) as m:
                    turn(m + skip, m, m)
            if last:
                last(TURNS - 1, main - 1, main - 1)
            if engine is nc.vector:
                engine.wait_ge(sum_done, main * GB)
                if head and head.counter:
                    head.decide(engine)
                engine.sem_inc(decided, 1)
            else:
                engine.wait_ge(decided, 1)
            n = engine.value_load(mem["passes"][0:1, 0:1], min_val=0, max_val=-(-N // WIN) + 1)
            with engine.If(n > 0):

                def opened(p):
                    if reset:
                        reset(p)
                    else:
                        wait_apart(engine, pass_open, p + 1, passed)

                opened(0)
                with engine.Fori(0, n) as p:
                    turn(0, p * TURNS + main, 0)
                    with engine.Fori(1, TURNS) as i:
                        turn(i, p * TURNS + main + i, i)
                    if last:
                        last(TURNS - 1, p * TURNS + main + TURNS - 1, TURNS - 1)
                    opened(p + 1)
                if undo:
                    undo(n)

        def met(engine, semaphore, count, m, r, apart=False):
            if isinstance(r, int) and count(r) <= 0:
                return
            if apart:
                wait_apart(engine, semaphore, count(m), passed)
            else:
                engine.wait_ge(semaphore, count(m))

        def nothing(half):
            pass

        @block.sync
        def _(sp):
            def turn(i, m, r, beside=nothing):
                for h in range(2):
                    for k in range(h * HG, h * HG + HG):
                        met(sp, rows_in[k], lambda j: j * 16 * TG, r, r, apart=True)
                    sp.dma_start(index[:, h, :], io["src"][ds(i * 2 + h, 1)].rearrange("a p t -> (a p) t")).then_inc(index_in[h], 16)
                    if edge_mlp:
                        met(sp, emb_done, lambda j: j * GB - GB + (h + 1) * HG, m, r, apart=True)
                        sp.dma_start(edges[:, h, :], io["edge_t"][ds(i * 2 + h, 1)].rearrange("a f e -> (a f) e")).then_inc(edges_in[h], 16)
                    beside(h)

            passes(sp, turn, lambda side, c, half: side.sync(sp, c, half))

        @block.gpsimd
        def _(pool):
            def turn(i, m, r, beside=nothing):
                for h in range(2):
                    met(pool, index_in[h], lambda j: j * 16 + 16, m, r, apart=True)
                    for k in range(h * HG, h * HG + HG):
                        met(pool, pre_ready if edge_mlp else seg_done, lambda j: j * GB - GB + k + 1, m, r, apart=True)
                        for t in range(TG):
                            at = (k - h * HG) * TG + t
                            pool.indirect_dma_start(rows[:, k, t, :], None, table,
                                                    bass.IndirectOffsetOnAxis(ap=index[:, h, at:at + 1], axis=0)
                                                    ).then_inc(rows_in[k], 16)

            def reset(p):
                wait_apart(pool, pass_done, p + 1, passed)
                landed = (TURNS - skip if isinstance(p, int) else TURNS) * 16 * TG
                pool.inc_swdge_sem(rows_in, [landed] * GB, mode="sub")
                pool.sem_inc(pass_open, 1)

            passes(pool, turn, lambda side, c, half: None, reset=reset)

        @block.scalar
        def _(act):
            def turn(i, m, r, beside=nothing):
                for k in range(GB):
                    if edge_mlp:
                        met(act, pre_ready, lambda j: j * GB + k + 1, m, r)
                        met(act, seg_done, lambda j: j * GB + k - 1, m, r)
                        act.activation(hid[:, k % 2], pre[:, k % 2], ACT.Relu).then_inc(hid_ready, 1)
                    if k % 4 == 1:
                        beside(k // 4)

            passes(act, turn, lambda side, c, half: side.scalar(act, c, half))

        @block.tensor
        def _(pe):
            def embed(m, r, k):
                if k % HG == 0:
                    met(pe, edges_in[k // HG], lambda j: j * 16 + 16, m, r)
                met(pe, pre_ready, lambda j: j * GB + k - 1, m, r)
                for t in range(TG):
                    at = ((k % HG) * TG + t) * P
                    mm = pe.matmul(emb_ps[k % 2][:, t * F:(t + 1) * F], edges[:, k // HG, at:at + P], mem["w1e"][:],
                                   start=True, stop=True)
                mm.then_inc(emb_done, 1)

            def segment(m, r, k):
                met(pe, hot_ready, lambda j: j * GB + k + 1, m, r)
                if edge_mlp:
                    met(pe, hid_ready, lambda j: j * GB + k + 1, m, r)
                else:
                    met(pe, rows_in[k], lambda j: j * 16 * TG + 16 * TG, r, r)
                met(pe, sum_done, lambda j: j * GB + k - 1, m, r)
                for t in range(TG):
                    values = hid[:, k % 2, t, :] if edge_mlp else rows[:, k, t, :]
                    mm = pe.matmul(seg_ps[k % 2][low:low + F, 0:WIN], values, hot[:, k % 4, t, :], start=(t == 0), stop=(t == TG - 1))
                mm.then_inc(seg_done, 1)

            def turn(i, m, r, beside=nothing):
                for k in range(GB):
                    if not edge_mlp:
                        segment(m, r, k)
                    else:
                        embed(m, r, k)
                        if k > 0 or not isinstance(r, int) or r > 0:
                            segment(m, r, k - 1)
                    if k % 4 == 1:
                        beside(k // 4)

            def between(k):
                if head and k == 0:
                    head.multiply(pe)
                if head and k == 3:
                    head.turn(pe)

            passes(pe, turn, lambda side, c, half: side.tensor(pe, c, half), between=between,
                   last=(lambda i, m, r: segment(m, r, GB - 1)) if edge_mlp else None)

        @block.vector
        def _(v):
            v.memset(mem["sums"][low:low + F, :], 0.0).then_inc(start, 1)
            v.tensor_copy(base[:], mem["base_row0"][:]).then_inc(start, 1)
            v.wait_ge(start, 2)

            def one_hot(i, m, r, k):
                met(v, seg_done, lambda j: j * GB + k - 3, m, r)
                v.tensor_tensor(hot[:, k % 4], mem["rel"][:, ds((i * GB + k) * TG, TG)].unsqueeze(2).broadcast_to([P, TG, WIN]),
                                mem["iota_f"][:, 0:WIN].unsqueeze(1).broadcast_to([P, TG, WIN]), ALU.is_equal).then_inc(hot_ready, 1)

            def add_parts(m, r, k):
                met(v, rows_in[k], lambda j: j * 16 * TG + 16 * TG, r, r)
                met(v, emb_done, lambda j: j * GB + k + 1, m, r)
                met(v, hid_ready, lambda j: j * GB + k - 1, m, r)
                v.tensor_tensor(pre[:, k % 2], emb_ps[k % 2][:].rearrange("p (t f) -> p t f", f=F), rows[:, k], ALU.add).then_inc(pre_ready, 1)

            def add_sums(i, m, r, k):
                first = v.value_load(base[0:1, ds(i * GB + k, 1)], min_val=0, max_val=N)
                met(v, seg_done, lambda j: j * GB + k + 1, m, r)
                met(v, sum_done, lambda j: j * GB + k, m, r)
                window = mem["sums"][low:low + F, ds(first, WIN)]
                v.tensor_tensor(window, window, seg_ps[k % 2][low:low + F, 0:WIN], ALU.add).then_inc(sum_done, 1)

            def turn(i, m, r, beside=nothing):
                for k in range(GB):
                    one_hot(i, m, r, k)
                    if edge_mlp:
                        add_parts(m, r, k)
                    if k > 0 or not isinstance(r, int) or r > 0:
                        add_sums(i, m, r, k - 1)
                    if k % 4 == 1:
                        beside(k // 4)

            def between(k):
                if not head:
                    return
                if k == 0 and head.counter:
                    head.counter.add(v, plan.HT * GB - 1)
                    v.wait_ge(head.counter.added, plan.HT * GB)
                    v.sem_inc(head.whole, 1)
                if k in (1, 2) and head.counter:
                    head.largest(v, k - 1)
                if k == 1:
                    head.add_parts(v)
                if k == 4:
                    head.finish(v, lambda: v.wait_ge(sum_done, (plan.CHUNKS + 12) * GB - 1))

            def reset(p):
                if isinstance(p, int):
                    v.memset(mem["sums"][low:low + F, :], 0.0).then_inc(moved, 1)
                    v.wait_ge(moved, 1)
                else:
                    v.wait_ge(sum_done, p * G + (TURNS - skip) * GB)
                    v.tensor_scalar(mem["rel"][:], mem["rel"][:], -float(WIN), None, ALU.add).then_inc(moved, 1)
                    v.tensor_scalar(base[:], base[:], WIN, N, ALU.add, ALU.min).then_inc(moved, 1)
                    v.wait_ge(moved, p * 2 + 1)
                v.sem_inc(pass_done, 1)
                v.wait_ge(pass_open, p + 1)

            def undo(n):
                with v.Fori(0, n) as p:
                    v.tensor_scalar(mem["rel"][:], mem["rel"][:], float(WIN), None, ALU.add).then_inc(start, 1)
                    v.wait_ge(start, p + 3)

            passes(v, turn, lambda side, c, half: side.vector(v, c, half), between=between,
                   last=lambda i, m, r: add_sums(i, m, r, GB - 1), reset=reset, undo=undo)


def over_chunks(engine, plan, step):
    assert plan.CHUNKS % 2 == 1
    for c in range(3):
        step(c, c % 2)
    with engine.Fori(1, plan.CHUNKS // 2) as j:
        step(j * 2 + 1, 1)
        step(j * 2 + 2, 0)


def second_table(nc, plan, mem, io):
    D, NB, NP, CB, CH = plan.D, plan.NB, plan.NP, plan.CB, plan.CHUNKS
    with ExitStack() as ctx:
        sem = lambda n: ctx.enter_context(nc.semaphore("t_" + n))
        part = [ctx.enter_context(nc.sbuf_tensor(f"t_part{q}", [D, CB, NP], F32)) for q in range(2)]
        rows_ps = [ctx.enter_context(nc.psum_tensor(f"t_rows_ps{q}", [P, 512], F32)) for q in range(2)]
        stage = ctx.enter_context(nc.sbuf_tensor("t_stage", [NP, NB, D], F32))
        picked, turned, scaled, out, passed = sem("picked"), sem("turned"), sem("scaled"), sem("out"), sem("passed")
        block = ctx.enter_context(nc.Block())
        sums = mem["sums"][0:D, 0:plan.N].rearrange("f (p b) -> f b p", b=NB)

        @block.scalar
        def _(act):
            def step(c, q):
                wait(act, turned, c - 1)
                act.copy(part[q][:], sums[:, ds(c * CB, CB), :]).then_inc(picked, 1)

            over_chunks(act, plan, step)

        @block.tensor
        def _(pe):
            def step(c, q):
                wait(pe, scaled, c - 1)
                wait_apart(pe, picked, c + 1, passed)
                for b in range(CB):
                    tr = pe.transpose(rows_ps[q][0:NP, b * D:(b + 1) * D], part[q][:, b, :], mem["ident"][0:D, 0:D])
                tr.then_inc(turned, 1)

            over_chunks(pe, plan, step)

        @block.vector
        def _(v):
            def step(c, q):
                v.wait_ge(turned, c + 1)
                v.tensor_tensor(stage[:, ds(c * CB, CB), :], rows_ps[q][0:NP, 0:CB * D].rearrange("p (b d) -> p b d", d=D),
                                mem["norm2"][:, ds(c * CB, CB)].unsqueeze(2).broadcast_to([NP, CB, D]), ALU.mult).then_inc(scaled, 1)

            over_chunks(v, plan, step)

        @block.sync
        def _(sp):
            table = io["table1"].rearrange("(p b) d -> p b d", b=NB)
            for a, b in plan.slices:
                sp.wait_ge(scaled, -(-b // CB))
                sp.dma_start(table[:, a:b, :], stage[:, a:b, :]).then_inc(out, 16)
            sp.wait_ge(out, 16 * len(plan.slices))


class LayerNorm:

    def __init__(self, ctx, nc, plan, tag, a):
        self.plan, self.a = plan, a
        self.sq = ctx.enter_context(nc.sbuf_tensor(tag + "sq", [plan.NP, plan.NB, plan.D], F32))
        self.stat = ctx.enter_context(nc.sbuf_tensor(tag + "stat", [plan.NP, 7, plan.NB], F32))
        sem = lambda n: ctx.enter_context(nc.semaphore(tag + n))
        self.chain, self.centred, self.squared, self.var_ready = sem("chain"), sem("centred"), sem("squared"), sem("var_ready")
        self.root_ready, self.rstd_ready, self.scaled, self.scaled_last = sem("root_ready"), sem("rstd_ready"), sem("scaled"), sem("scaled_last")
        self.count = 0

    def link(self, v, ins):
        self.count += 1
        ins.then_inc(self.chain, 1)
        v.wait_ge(self.chain, self.count)

    def wide(self, k, a, b):
        return self.stat[:, k, a:b].unsqueeze(2).broadcast_to([self.plan.NP, b - a, self.plan.D])

    def centre(self, v, a, b):
        t, D = self.a[:, a:b, :], self.plan.D
        self.link(v, v.tensor_reduce(self.stat[:, 0, a:b], t, AX.X, ALU.add))
        self.link(v, v.tensor_scalar(self.stat[:, 1, a:b], self.stat[:, 0, a:b], -1.0 / D, None, ALU.mult))
        v.tensor_tensor(t, t, self.wide(1, a, b), ALU.add).then_inc(self.centred, 1)

    def variance(self, v, n, a, b):
        v.wait_ge(self.squared, n + 1)
        self.link(v, v.tensor_reduce(self.stat[:, 2, a:b], self.sq[:, a:b, :], AX.X, ALU.add))
        v.tensor_scalar(self.stat[:, 3, a:b], self.stat[:, 2, a:b], 1.0 / self.plan.D, EPS, ALU.mult, ALU.add).then_inc(self.var_ready, 1)

    def rstd(self, v, n, a, b):
        s = lambda k: self.stat[:, k, a:b]
        v.wait_ge(self.root_ready, n + 1)
        self.link(v, v.reciprocal(s(5), s(4)))
        self.link(v, v.tensor_tensor(s(6), s(5), s(5), ALU.mult))
        self.link(v, v.tensor_tensor(s(6), s(6), s(3), ALU.mult))
        self.link(v, v.tensor_scalar(s(6), s(6), -0.5, 1.5, ALU.mult, ALU.add))
        v.tensor_tensor(s(5), s(6), s(5), ALU.mult).then_inc(self.rstd_ready, 1)

    def vector(self, v, ready=None):
        slices = self.plan.slices
        n = len(slices)
        for k in range(n + 2):
            if k < n:
                if ready:
                    ready(slices[k][1])
                self.centre(v, *slices[k])
            if 1 <= k <= n:
                self.variance(v, k - 1, *slices[k - 1])
            if k >= 2:
                self.rstd(v, k - 2, *slices[k - 2])
        a, b = slices[-1]
        v.wait_ge(self.rstd_ready, n)
        v.tensor_tensor(self.a[:, a:b, :], self.a[:, a:b, :], self.wide(5, a, b), ALU.mult).then_inc(self.scaled_last, 1)

    def square(self, act, k):
        a, b = self.plan.slices[k]
        act.wait_ge(self.centred, k + 1)
        act.activation(self.sq[:, a:b, :], self.a[:, a:b, :], ACT.Square).then_inc(self.squared, 1)

    def root(self, act, k):
        a, b = self.plan.slices[k]
        act.wait_ge(self.var_ready, k + 1)
        act.activation(self.stat[:, 4, a:b], self.stat[:, 3, a:b], ACT.Sqrt).then_inc(self.root_ready, 1)

    def scalar(self, act):
        for k in range(len(self.plan.slices) + 1):
            if k < len(self.plan.slices):
                self.square(act, k)
            if k > 0:
                self.root(act, k - 1)

    def gpsimd(self, pool):
        for k, (a, b) in enumerate(self.plan.slices[:-1]):
            pool.wait_ge(self.rstd_ready, k + 1)
            pool.tensor_tensor(self.a[:, a:b, :], self.a[:, a:b, :], self.wide(5, a, b), ALU.mult).then_inc(self.scaled, 1)
        pool.wait_ge(self.scaled, len(self.plan.slices) - 1)


def first_layer(nc, plan, mem, io):
    N, D, H, NB, NP, CB, CH = plan.N, plan.D, plan.H, plan.NB, plan.NP, plan.CB, plan.CHUNKS
    with ExitStack() as ctx:
        sb = lambda n, s: ctx.enter_context(nc.sbuf_tensor("f_" + n, s, F32))
        ps = lambda n: ctx.enter_context(nc.psum_tensor("f_" + n, [P, 512], F32))
        sem = lambda n: ctx.enter_context(nc.semaphore("f_" + n))
        part = [sb(f"part{q}", [P, CB, NP]) for q in range(2)]
        part_n = sb("part_n", [NP, CB, D])
        x1_t = [sb(f"x1_t{q}", [D + 1, CB, NP]) for q in range(2)]
        rows3 = [sb(f"rows3{q}", [NP, CB, H]) for q in range(2)]
        hop_ps, turn_ps, tab_ps = ([ps(f"{n}{q}") for q in range(2)] for n in ("hop_ps", "turn_ps", "tab_ps"))
        xr = mem["xr"][:].rearrange("p (b d) -> p b d", d=D)
        norm = LayerNorm(ctx, nc, plan, "f_", xr)
        picked, mixed, scaled, summed, ones = sem("picked"), sem("mixed"), sem("scaled_hop"), sem("summed"), sem("ones")
        handed, turned, copied, tab_done, tab_ready, passed = sem("handed"), sem("turned"), sem("copied"), sem("tab_done"), sem("tab_ready"), sem("passed")
        out = [sem(f"out{q}") for q in range(2)]
        x1_in = [sb(f"x1_in{q}", [NP, CB, D]) for q in range(2)]
        block = ctx.enter_context(nc.Block())
        sums = mem["sums"][D:2 * D, 0:N].rearrange("f (p b) -> f b p", b=NB)
        table = io["table2"].rearrange("(p b) h -> p b h", b=NB)

        @block.sync
        def _(sp):
            def step(c, q):
                wait_apart(sp, tab_ready, c + 1, passed)
                sp.dma_start(table[:, ds(c * CB, CB), :], rows3[q][:]).then_inc(out[q], 16)

            over_chunks(sp, plan, step)
            sp.wait_ge(out[0], 16 * (CH // 2 + 1))
            sp.wait_ge(out[1], 16 * (CH // 2))

        @block.gpsimd
        def _(pool):
            norm.gpsimd(pool)

            def step(c, q):
                wait(pool, turned, c - 1)
                pool.tensor_copy(x1_in[q][:], xr[:, ds(c * CB, CB), :]).then_inc(handed, 1)

            pool.wait_ge(norm.scaled_last, 1)
            over_chunks(pool, plan, step)

        @block.scalar
        def _(act):
            def pick(c, q):
                wait(act, mixed, c - 1)
                act.copy(part[q][D:2 * D], sums[:, ds(c * CB, CB), :]).then_inc(picked, 1)

            over_chunks(act, plan, pick)
            norm.scalar(act)

            def copy(c, q):
                act.wait_ge(turned, c + 1)
                wait(act, tab_done, c - 1)
                act.copy(x1_t[q][0:D], turn_ps[q][0:D, 0:CB * NP].rearrange("f (b p) -> f b p", p=NP)).then_inc(copied, 1)

            over_chunks(act, plan, copy)

        @block.tensor
        def _(pe):
            def mix(c, q):
                wait(pe, scaled, c - 1)
                pe.wait_ge(picked, c + 1)
                for b in range(CB):
                    mm = pe.matmul(hop_ps[q][0:NP, b * D:(b + 1) * D], part[q][D:2 * D, b, :], mem["w12"][D:2 * D], start=True, stop=True)
                mm.then_inc(mixed, 1)

            over_chunks(pe, plan, mix)
            pe.wait_ge(ones, 2)

            def turn(c, q):
                wait(pe, copied, c - 1)
                wait_apart(pe, handed, c + 1, passed)
                for b in range(CB):
                    tr = pe.transpose(turn_ps[q][0:D, b * NP:(b + 1) * NP], x1_in[q][:, b, :], mem["ident"][0:NP, 0:NP])
                tr.then_inc(turned, 1)

            def tab(c, q):
                pe.wait_ge(copied, c + 1)
                wait(pe, tab_ready, c - 1)
                for b in range(CB):
                    mm = pe.matmul(tab_ps[q][0:NP, b * H:(b + 1) * H], x1_t[q][:, b, :], mem["w1x"][:], start=True, stop=True)
                mm.then_inc(tab_done, 1)

            turn(0, 0)
            for c in range(3):
                turn(c + 1, (c + 1) % 2)
                tab(c, c % 2)
            with pe.Fori(1, CH // 2 - 1) as j:
                for k in (1, 2):
                    turn(j * 2 + k + 1, (k + 1) % 2)
                    tab(j * 2 + k, k % 2)
            turn(CH - 1, 0)
            tab(CH - 2, 1)
            tab(CH - 1, 0)

        @block.vector
        def _(v):
            v.memset(x1_t[0][D:D + 1], 1.0).then_inc(ones, 1)
            v.memset(x1_t[1][D:D + 1], 1.0).then_inc(ones, 1)

            def step(c, q):
                at = ds(c * CB, CB)
                v.wait_ge(mixed, c + 1)
                wait(v, summed, c)
                v.tensor_tensor(part_n[:], hop_ps[q][0:NP, 0:CB * D].rearrange("p (b d) -> p b d", d=D),
                                mem["norm"][:, at].unsqueeze(2).broadcast_to([NP, CB, D]), ALU.mult).then_inc(scaled, 1)
                v.wait_ge(scaled, c + 1)
                v.tensor_tensor(xr[:, at, :], xr[:, at, :], part_n[:], ALU.add).then_inc(summed, 1)

            over_chunks(v, plan, step)
            v.wait_ge(summed, CH)
            norm.vector(v)

            def copy(c, q, store):
                v.wait_ge(tab_done, c + 1)
                wait(v, out[q], store)
                v.tensor_copy(rows3[q][:], tab_ps[q][0:NP, 0:CB * H].rearrange("p (b h) -> p b h", h=H)).then_inc(tab_ready, 1)

            for c in range(3):
                copy(c, c % 2, 16 * (c // 2))
            with v.Fori(1, CH // 2) as j:
                copy(j * 2 + 1, 1, j * 16)
                copy(j * 2 + 2, 0, j * 16 + 16)


def second_layer(nc, plan, mem, io):
    N, D, H, NB, NP, CB, CH = plan.N, plan.D, plan.H, plan.NB, plan.NP, plan.CB, plan.CHUNKS
    with ExitStack() as ctx:
        sb = lambda n, s: ctx.enter_context(nc.sbuf_tensor("s_" + n, s, F32))
        ps = lambda n: ctx.enter_context(nc.psum_tensor("s_" + n, [P, 512], F32))
        sem = lambda n: ctx.enter_context(nc.semaphore("s_" + n))
        part = [sb(f"part{q}", [P, CB, NP]) for q in range(2)]
        cat = [sb(f"cat{q}", [NP, CB, 2 * D]) for q in range(2)]
        agg_n = sb("agg_n", [NP, CB, D])
        cat_t = [sb(f"cat_t{q}", [2 * D, CB, NP]) for q in range(2)]
        hid_t = [sb(f"hid_t{q}", [D + 1, CB, NP]) for q in range(2)]
        c3 = sb("c3", [D, 1])
        agg_ps, turn_ps, hid_ps, out_ps = ([ps(f"{n}{q}") for q in range(2)] for n in ("agg_ps", "turn_ps", "hid_ps", "out_ps"))
        xr = mem["xr"][:].rearrange("p (b d) -> p b d", d=D)
        norm = LayerNorm(ctx, nc, plan, "s_", xr)
        picked, agg_done, agg_scaled, cat_ready, x1_ready = sem("picked"), sem("agg_done"), sem("agg_scaled"), sem("cat_ready"), sem("x1_ready")
        turned, copied, hid_done, hid_ready, mlp_done, summed = sem("turned"), sem("copied"), sem("hid_done"), sem("hid_ready"), sem("mlp_done"), sem("summed")
        c3_done, start, out, passed = sem("c3_done"), sem("start"), sem("out"), sem("passed")
        block = ctx.enter_context(nc.Block())
        sums = mem["sums"][:, 0:N].rearrange("f (p b) -> f b p", b=NB)
        add2 = mem["add2"][:].rearrange("p (b d) -> p b d", d=D)
        out_dram = io["out"].rearrange("(p b) d -> p b d", b=NB)
        flat = lambda bank: bank[0:NP, 0:CB * D].rearrange("p (b d) -> p b d", d=D)

        @block.sync
        def _(sp):
            for k, (a, b) in enumerate(plan.slices):
                if k < len(plan.slices) - 1:
                    sp.wait_ge(norm.scaled, k + 1)
                else:
                    sp.wait_ge(norm.scaled_last, 1)
                sp.dma_start(out_dram[:, a:b, :], xr[:, a:b, :]).then_inc(out, 16)
            sp.wait_ge(out, 16 * len(plan.slices))

        @block.gpsimd
        def _(pool):
            def step(c, q):
                wait(pool, turned, c - 1)
                pool.tensor_copy(cat[q][:, :, 0:D], xr[:, ds(c * CB, CB), :]).then_inc(x1_ready, 1)

            over_chunks(pool, plan, step)
            norm.gpsimd(pool)

        @block.scalar
        def _(act):
            act.wait_ge(start, 3)

            def pick(c, q):
                wait(act, agg_done, c - 1)
                act.copy(part[q][:], sums[:, ds(c * CB, CB), :]).then_inc(picked, 1)

            def copy(c, q):
                act.wait_ge(turned, c + 1)
                wait(act, hid_done, c - 1)
                act.copy(cat_t[q][:], turn_ps[q][:, 0:CB * NP].rearrange("f (b p) -> f b p", p=NP)).then_inc(copied, 1)

            def relu(c, q):
                act.wait_ge(hid_done, c + 1)
                wait(act, mlp_done, c - 1)
                act.activation(hid_t[q][0:D], hid_ps[q][0:D, 0:CB * NP].rearrange("f (b p) -> f b p", p=NP), ACT.Relu,
                               bias=c3[:]).then_inc(hid_ready, 1)

            staggered(act, plan, [pick, copy, relu])
            norm.scalar(act)

        @block.tensor
        def _(pe):
            pe.matmul(out_ps[0][0:D, 0:1], mem["w3u"][:], mem["u0"][:], start=True, stop=True).then_inc(c3_done, 1)
            pe.wait_ge(start, 3)

            def agg(c, q):
                wait(pe, agg_scaled, c - 1)
                pe.wait_ge(picked, c + 1)
                for b in range(CB):
                    mm = pe.matmul(agg_ps[q][0:NP, b * D:(b + 1) * D], part[q][:, b, :], mem["w2"][:], start=True, stop=True)
                mm.then_inc(agg_done, 1)

            def turn(c, q):
                wait(pe, copied, c - 1)
                pe.wait_ge(x1_ready, c + 1)
                wait_apart(pe, cat_ready, c + 1, passed)
                for b in range(CB):
                    tr = pe.transpose(turn_ps[q][:, b * NP:(b + 1) * NP], cat[q][:, b, :], mem["ident"][0:NP, 0:NP])
                tr.then_inc(turned, 1)

            def hid(c, q):
                wait(pe, hid_ready, c - 1)
                pe.wait_ge(copied, c + 1)
                pe.matmul(hid_ps[q][0:D, 0:CB * NP], mem["w3xa"][:], cat_t[q][:].rearrange("f b p -> f (b p)"),
                          start=True, stop=True).then_inc(hid_done, 1)

            def mlp(c, q):
                wait(pe, summed, c - 1)
                pe.wait_ge(hid_ready, c + 1)
                for b in range(CB):
                    mm = pe.matmul(out_ps[q][0:NP, b * D:(b + 1) * D], hid_t[q][:, b, :], mem["w4"][:], start=True, stop=True)
                mm.then_inc(mlp_done, 1)

            staggered(pe, plan, [agg, turn, hid, mlp])

        @block.vector
        def _(v):
            v.memset(hid_t[0][D:D + 1], 1.0).then_inc(start, 1)
            v.memset(hid_t[1][D:D + 1], 1.0).then_inc(start, 1)
            v.wait_ge(c3_done, 1)
            v.tensor_tensor(c3[:], out_ps[0][0:D, 0:1], mem["b3"][:], ALU.add).then_inc(start, 1)

            def agg(c, q):
                v.wait_ge(agg_done, c + 1)
                wait(v, cat_ready, c)
                v.tensor_tensor(agg_n[:], flat(agg_ps[q]), mem["inv"][:, ds(c * CB, CB)].unsqueeze(2).broadcast_to([NP, CB, D]),
                                ALU.mult).then_inc(agg_scaled, 1)
                wait(v, turned, c - 1)
                v.wait_ge(agg_scaled, c + 1)
                v.tensor_tensor(cat[q][:, :, D:2 * D], agg_n[:], add2[:, ds(c * CB, CB), :], ALU.add).then_inc(cat_ready, 1)

            def add(c, q):
                v.wait_ge(mlp_done, c + 1)
                v.wait_ge(x1_ready, c + 1)
                at = xr[:, ds(c * CB, CB), :]
                v.tensor_tensor(at, at, flat(out_ps[q]), ALU.add).then_inc(summed, 1)

            staggered(v, plan, [agg, add], lags=[0, 3])
            v.wait_ge(summed, CH)
            norm.vector(v)


def staggered(engine, plan, stages, lags=None):
    n = plan.CHUNKS
    lags = lags or list(range(len(stages)))
    most = lags[-1]

    def turn(c, among=None):
        for stage, lag in reversed(list(zip(stages, lags))):
            if among is None or 0 <= c - lag < n:
                parity = (among if among is not None else turn.parity) - lag
                stage(c - lag, parity % 2)

    head = most + 3
    pairs = (n - head) // 2
    for c in range(head):
        turn(c, among=c)
    with engine.Fori(0, pairs) as j:
        for k in range(2):
            turn.parity = head + k
            turn(j * 2 + head + k)
    for c in range(head + 2 * pairs, n + most):
        turn(c, among=c)


def build(nc, plan, io):
    N, D, NB, NP, T, G, H = plan.N, plan.D, plan.NB, plan.NP, plan.T, plan.G, plan.H
    HT = plan.HT * plan.TG * plan.GB
    F16 = mybir.dt.float16
    with ExitStack() as ctx:
        mem = {}

        def place(stack, *tensors):
            for name, shape, dt in tensors:
                mem[name] = stack.enter_context(nc.sbuf_tensor("m_" + name, shape, dt))

        place(
            ctx,
            ("xr", [NP, NB * D], F32),
            ("sums", [P, N + plan.WIN], F32),
            ("rel", [P, T], F32),
            ("base_row0", [1, G], I32),
            ("passes", [1, 1], I32), ("passes_any", [1, 1], I32),
            ("extremes", [1, 3], F32),
            ("limits", [1, 4], F32),
            ("iota_f", [P, P], F32),
            ("norm", [NP, NB], F32), ("norm2", [NP, NB], F32),
            ("inv", [NP, NB], F32), ("some", [NP, NB], F32),
            ("ident", [P, P], F32),
            ("w0", [D, D], F32), ("w12", [2 * D, D], F32), ("bias0", [P, D], F32),
            ("w1x", [D + 1, H], F32), ("w1e", [plan.FE, H], F32),
            ("w2", [H, D], F32), ("b2", [P, D], F32),
            ("w3xa", [2 * D, D], F32), ("w3u", [D, D], F32), ("b3", [D, 1], F32),
            ("w4", [D + 1, D], F32), ("u0", [D, 1], F32),
        )
        with ExitStack() as hops:
            place(
                hops,
                ("counts", [NP, NB, plan.HN + plan.HW], BF16),
                ("head_p", [P, HT], F32), ("head_b", [P, HT], F32),
                ("base_head", [1, HT // plan.TG], I32),
                ("iota_2", [P, NB * plan.HW], F16),
            )
            prologue(nc, plan, mem, io)
            with ExitStack() as hop:
                mem["parts"] = hop.enter_context(nc.sbuf_tensor("parts1", [NP, NB, 3, D], BF16))
                mem["banks"] = hop.enter_context(nc.psum_tensor("banks1", [P, 4, 512], F32))
                edge_sums(nc, plan, mem, io, "h1_", io["table0"], 0, [OwnPart, TableParts, HeadCounts])
            second_table(nc, plan, mem, io)
            with ExitStack() as hop:
                mem["parts"] = hop.enter_context(nc.sbuf_tensor("parts2", [NP, NB, 3, D], BF16))
                mem["banks"] = hop.enter_context(nc.psum_tensor("banks2", [P, 4, 512], F32))
                edge_sums(nc, plan, mem, io, "h2_", io["table1"], D, [FirstHopPart, TableParts])
        first_layer(nc, plan, mem, io)
        place(ctx, ("add2", [NP, NB * D], F32))
        edge_sums(nc, plan, mem, io, "e_", io["table2"], 0, [MeanBias], edge_mlp=True)
        second_layer(nc, plan, mem, io)


def kernel(**inputs):
    import numpy as np
    import concourse.bacc as bacc
    from concourse.bass_utils import run_bass_kernel_spmd

    x, src, dst, edge = (np.asarray(inputs[k]) for k in ("x", "src", "dst", "edge_attr_32"))
    w, b0, u, w3 = (np.asarray(inputs[k]) for k in ("L0_gnn_weight", "L0_gnn_bias", "L1_gnn_u", "L1_gnn_W3"))
    w1, b1, w2, b2, b3, w4, b4 = (np.asarray(inputs["L1_gnn_" + k]) for k in ("W1", "b1", "W2", "b2", "b3", "W4", "b4"))
    N, D = x.shape
    E, FE = edge.shape
    plan = Plan(N, E, D, FE, w1.shape[1])
    NB, NP, T, TH = plan.NB, plan.NP, plan.T, plan.TH
    pad = T * P - E
    src_p = np.concatenate([src, np.zeros(pad, src.dtype)])
    dst_p = np.concatenate([dst, np.full(pad, N, dst.dtype)])
    edge_p = np.concatenate([edge, np.zeros((pad, FE), edge.dtype)])
    rows = lambda a: np.ascontiguousarray(np.broadcast_to(a, (P, a.shape[0])))
    arrays = {
        "x": x,
        "x_t": x.reshape(NP, NB, D).transpose(2, 1, 0).reshape(D, N),
        "src": src_p.reshape(T // TH, TH, P).transpose(0, 2, 1),
        "dst": dst_p.reshape(T, P).T,
        "edge_t": edge_p.reshape(T // TH, TH * P, FE).transpose(0, 2, 1),
        "ident": np.eye(P, dtype=x.dtype),
        "w0": w[:, 0:D].T, "w12": w[:, D:3 * D].T, "bias0": rows(b0),
        "w1x": np.concatenate([w1[0:D], b1[None]]), "w1e": w1[D:D + FE],
        "w2": w2, "b2": rows(b2),
        "w3xa": w3[0:2 * D], "w3u": w3[2 * D:3 * D], "b3": b3[:, None],
        "w4": np.concatenate([w4, b4[None]]), "u0": u[0][:, None],
    }
    arrays = {"in_" + k: np.ascontiguousarray(a) for k, a in arrays.items()}
    nc = bacc.Bacc("TRN2", target_bir_lowering=False, num_devices=1)
    io = {k[3:]: nc.dram_tensor(k, a.shape, mybir.dt.from_np(a.dtype), kind="ExternalInput").ap() for k, a in arrays.items()}
    io["out"] = nc.dram_tensor("out_0", (N, D), F32, kind="ExternalOutput").ap()
    for name, shape, dt in (("table0", (N, D), F32), ("table1", (N, D), F32), ("table2", (N, plan.H), F32), ("scratch_base", (plan.G,), I32)):
        io[name] = nc.dram_tensor(name, shape, dt, kind="Internal").ap()
    build(nc, plan, io)
    r = run_bass_kernel_spmd(nc, [arrays], core_ids=[0])
    return r.results[0]["out_0"]
```

```python
from contextlib import ExitStack

import concourse.bass as bass
from concourse import mybir

ALU = mybir.AluOpType
ACT = mybir.ActivationFunctionType
AX = mybir.AxisListType
F32 = mybir.dt.float32
BF16 = mybir.dt.bfloat16
I32 = mybir.dt.int32

P = 128
EPS = 1e-5


class Region:

    def __init__(self, plan, turn, turns, origin, width, counted, slots, again):
        self.turn, self.turns, self.origin, self.width, self.slots, self.again = turn, turns, origin, width, slots, again
        self.tiles = (turn * plan.TG * plan.GB, (turn + turns) * plan.TG * plan.GB)
        self.groups = (turn * plan.GB, (turn + turns) * plan.GB)
        self.counted, self.whole = counted, counted + 1 + turns * plan.GB // slots


class Plan:

    def __init__(self, nodes, edges, feat, edge_feat, hidden):
        self.N, self.E, self.D, self.FE, self.H = nodes, edges, feat, edge_feat, hidden
        self.NB = 100
        self.NP = nodes // self.NB
        assert self.NP * self.NB == nodes and self.NP <= P
        self.TG = 4
        self.GB = 8
        self.TH = self.TG * self.GB // 2
        per_turn = P * self.TG * self.GB
        self.TURNS = -(-edges // per_turn)
        self.T = self.TURNS * self.TG * self.GB
        self.G = self.TURNS * self.GB
        self.REAL = -(-edges // P)
        self.WIN = 128
        self.HN = 360
        self.HQ = self.HN // 4
        self.SLOTS = self.GB // 2
        self.PB = 10
        self.PT = self.NB // self.PB // 2
        self.regions = [Region(self, 0, 8, 0, 14, 0, 4, 8)]
        self.regions.append(Region(self, 8, 3, 316, 20, self.regions[0].whole + self.PT, 3, 1))
        self.HT = sum(r.turns for r in self.regions)
        self.HW = max(r.width for r in self.regions)
        self.CB = 4
        self.CHUNKS = self.NB // self.CB
        self.norm_ends = [8, 16, 22, self.CHUNKS]
        assert self.CHUNKS == 25
        step = self.NB // 4
        self.slices = [(a, a + step) for a in range(0, self.NB, step)]


def ds(start, size):
    return bass.ds(start, size)


def wait(engine, semaphore, value):
    if not isinstance(value, int) or value > 0:
        engine.wait_ge(semaphore, value)


def wait_apart(engine, semaphore, value, passed):
    if not isinstance(value, int):
        engine.wait_ge(semaphore, value)
        engine.sem_inc(passed, 1)
    elif value > 0:
        engine.wait_ge(semaphore, value)


def prologue(nc, plan, mem, io):
    N, D, NB, NP, T, G, TG = plan.N, plan.D, plan.NB, plan.NP, plan.T, plan.G, plan.TG
    U = 16
    HT = plan.HT * plan.TG * plan.GB
    HB = 2
    GC = G // 4
    with ExitStack() as ctx:
        sb = lambda n, s, d: ctx.enter_context(nc.sbuf_tensor(n, s, d))
        ps = lambda n, s, d: ctx.enter_context(nc.psum_tensor(n, s, d))
        sem = lambda n: ctx.enter_context(nc.semaphore(n))
        dst_i = sb("dst_i", [P, T], I32)
        dst_f = sb("dst_f", [P, T], F32)
        hi_i = sb("hi_i", [P, T], I32)
        digit_hi = sb("digit_hi", [P, HT], F32)
        digit_hi2 = sb("digit_hi2", [P, T], F32)
        digit_lo = sb("digit_lo", [P, T], F32)
        fix = sb("fix", [P, T], F32)
        hi_b = sb("hi_b", [P, T], BF16)
        lo_b = sb("lo_b", [P, T], BF16)
        iota_i = sb("iota_i", [P, P], I32)
        iota_head = mem["sums"][:, NB * D:NB * (D + plan.HW)].bitcast(I32)
        iota_b = sb("iota_b", [P, NP, U], BF16)
        one_hi = sb("one_hi", [P, HB, NP, U], BF16)
        one_lo = sb("one_lo", [P, HB, NB, U], BF16)
        stage = mem["sums"][0:NP, 0:NB * D].rearrange("p (b d) -> p b d", d=D)
        deg = sb("deg", [NP, NB], F32)
        tmp = sb("tmp", [NP, NB], F32)
        tmp2 = sb("tmp2", [NP, NB], F32)
        least = sb("least", [P, G], F32)
        least_t = sb("least_t", [GC, 4], F32)
        least_i = sb("least_i", [GC, 4], I32)
        base_bc = sb("base_bc", [P, G], F32)
        base_bi = sb("base_bi", [P, G], I32)
        far = sb("far", [P, 6], F32)
        far_i = sb("far_i", [1, 1], I32)
        head_src = sb("head_src", [P, plan.HT * 2, plan.TH], I32)
        deg_ps = ps("deg_ps", [NP, 512], F32)
        tr_ps = ps("tr_ps", [P, 1024], F32)

        loaded = sem("p_loaded")
        iota_ready = sem("p_iota")
        dve = sem("p_dve")
        hot_ready = sem("p_hot_ready")
        hot_used = sem("p_hot_used")
        turned = sem("p_turned")
        scaled = sem("p_sqrt")
        spread = sem("p_spread")
        table_out = sem("p_table_out")
        table_ready = sem("p_table_ready")
        x_loaded = sem("p_x_loaded")
        w_loaded = sem("p_w_loaded")
        marks = {}

        block = ctx.enter_context(nc.Block())

        @block.vector
        def _(v):
            count = [0]

            def link(ins, mark=None):
                count[0] += 1
                ins.then_inc(dve, 1)
                v.wait_ge(dve, count[0])
                if mark:
                    marks[mark] = count[0]

            def digits(a, n, hi, lo):
                q, h, l, f = hi_i[:, 0:n], digit_hi2[:, 0:n], digit_lo[:, 0:n], fix[:, 0:n]
                link(v.tensor_scalar(l, a, 1.0 / NB, 0.5 / NB - 0.5, ALU.mult, ALU.add))
                link(v.tensor_copy(q, l))
                link(v.tensor_copy(h, q))
                link(v.scalar_tensor_tensor(out=l, in0=h, scalar=-float(NB), in1=a, op0=ALU.mult, op1=ALU.add))
                link(v.tensor_scalar(f, l, float(NB), None, ALU.is_ge))
                link(v.tensor_tensor(hi, h, f, ALU.add))
                link(v.scalar_tensor_tensor(out=lo, in0=f, scalar=-float(NB), in1=l, op0=ALU.mult, op1=ALU.add))

            v.wait_ge(iota_ready, 2)
            link(v.tensor_copy(mem["iota_2"][:], iota_head))
            link(v.tensor_copy(iota_b[:], iota_i[:, 0:NP].unsqueeze(2).broadcast_to([P, NP, U])))
            link(v.tensor_copy(mem["iota_f"][:], iota_i[:]))
            v.wait_ge(loaded, 16)
            link(v.tensor_copy(dst_f[:], dst_i[:]))
            digits(dst_f[:], T, hi_b[:], lo_b[:])

            def hot(n, k):
                wait(v, hot_used, n - HB + 1)
                tiles = lambda a, w: a[:, ds(n * U, U)].unsqueeze(1).broadcast_to([P, w, U])
                v.tensor_tensor(one_hi[:, k], tiles(hi_b, NP), iota_b[:], ALU.is_equal)
                v.tensor_tensor(one_lo[:, k], tiles(lo_b, NB), iota_b[:, 0:NB], ALU.is_equal).then_inc(hot_ready, 1)

            for k in range(HB):
                hot(k, k)
            link(v.tensor_reduce(least[:], dst_f[:].rearrange("p (g t) -> p g t", t=TG), AX.X, ALU.min), "least")
            third = T // U // HB // 3
            for a, b in ((1, 2 * third), (2 * third, T // U // HB)):
                with v.Fori(a, b) as i:
                    for k in range(HB):
                        hot(i * HB + k, k)
                if a == 1:
                    v.wait_ge(turned, 1)
                    link(v.tensor_reduce(least_t[:], tr_ps[0:GC, 0:4 * P].rearrange("q (c p) -> q c p", p=P), AX.X, ALU.min))
                    link(v.tensor_copy(least_i[:], least_t[:]), "least_i")

            v.wait_ge(hot_used, T // U)
            link(v.tensor_copy(deg[:], deg_ps[:, 0:NB]))
            link(v.tensor_scalar(tmp[:], deg[:], 1.0, None, ALU.max), "deg_max")
            link(v.reciprocal(mem["inv"][:], tmp[:]))
            link(v.tensor_tensor(mem["some"][:], deg[:], mem["inv"][:], ALU.mult))
            v.wait_ge(scaled, 1)
            link(v.reciprocal(mem["norm"][:], tmp2[:]))
            link(v.tensor_tensor(tmp2[:], mem["norm"][:], mem["norm"][:], ALU.mult))
            link(v.tensor_tensor(tmp2[:], tmp2[:], tmp[:], ALU.mult))
            link(v.tensor_scalar(tmp2[:], tmp2[:], -0.5, 1.5, ALU.mult, ALU.add))
            link(v.tensor_tensor(mem["norm"][:], tmp2[:], mem["norm"][:], ALU.mult))
            link(v.tensor_tensor(mem["norm2"][:], mem["norm"][:], mem["norm"][:], ALU.mult))
            v.wait_ge(x_loaded, 32)
            for a, b in plan.slices:
                v.tensor_tensor(stage[:, a:b, :], mem["xr"][:].rearrange("p (b d) -> p b d", d=D)[:, a:b, :],
                                mem["norm"][:, a:b].unsqueeze(2).broadcast_to([NP, b - a, D]), ALU.mult).then_inc(table_ready, 1)

            v.wait_ge(spread, 48)
            link(v.tensor_copy(base_bc[:], base_bi[:]))
            link(v.tensor_tensor(mem["rel"][:].rearrange("p (g t) -> p g t", t=TG), dst_f[:].rearrange("p (g t) -> p g t", t=TG),
                                 base_bc[:].unsqueeze(2).broadcast_to([P, G, TG]), ALU.subtract))
            link(v.tensor_reduce(far[:, 0:1], mem["rel"][:], AX.X, ALU.max))
            for k, r in enumerate(plan.regions):
                a, b = r.tiles
                link(v.tensor_reduce(far[:, k + 1:k + 2], mem["rel"][:, a:b], AX.X, ALU.max))
                link(v.tensor_reduce(far[:, k + 3:k + 4], dst_f[:, a:b], AX.X, ALU.max))
            a, b = plan.regions[1].tiles
            link(v.tensor_reduce(far[:, 5:6], dst_f[:, a:b], AX.X, ALU.min))
            link(v.tensor_scalar(far[:, 5:6], far[:, 5:6], -1.0, None, ALU.mult), "far")
            for r in plan.regions:
                a, b = r.groups
                link(v.tensor_scalar(mem["base_head"][:, a:b], mem["base_row0"][:, a:b], -r.origin, 0, ALU.add, ALU.max))
                link(v.tensor_scalar(mem["base_head"][:, a:b], mem["base_head"][:, a:b], plan.HN, None, ALU.min))
            v.wait_ge(x_loaded, 32)
            link(v.tensor_copy(digit_hi[:, 0:HT], head_src[:].rearrange("p h t -> p (h t)")))
            digits(digit_hi[:, 0:HT], HT, mem["head_p"][:], mem["head_b"][:])
            for r in plan.regions:
                at = slice(*r.tiles)
                link(v.tensor_scalar(fix[:, at], mem["rel"][:, at], float(r.width), float(NB * plan.HW), ALU.is_ge, ALU.mult))
                link(v.tensor_tensor(fix[:, at], fix[:, at], mem["rel"][:, at], ALU.add))
                link(v.scalar_tensor_tensor(out=mem["head_b"][:, at], in0=mem["head_b"][:, at], scalar=float(r.width), in1=fix[:, at], op0=ALU.mult, op1=ALU.add))
            v.wait_ge(turned, 2)
            link(v.tensor_reduce(mem["extremes"][:], tr_ps[0:1, 0:6 * P].rearrange("a (k p) -> a k p", p=P), AX.X, ALU.max))
            link(v.tensor_copy(far_i[:], mem["extremes"][:, 0:1]))
            link(v.tensor_scalar(far_i[:], far_i[:], 7, None, ALU.arith_shift_right))
            link(v.tensor_scalar(mem["passes_any"][:], far_i[:], 1, None, ALU.add))
            for k, limit in enumerate((plan.WIN, *(r.width for r in plan.regions), *(r.origin + plan.HN for r in plan.regions),
                                       1 - plan.regions[1].origin, 256)):
                link(v.memset(mem["limits"][:, k:k + 1], float(limit)))

        @block.sync
        def _(sp):
            sp.dma_start(dst_i[:], io["dst"]).then_inc(loaded, 16)
            sp.dma_start(head_src[:], io["src"][0:plan.HT * 2].rearrange("h p t -> p h t")).then_inc(x_loaded, 16)
            sp.dma_start(mem["xr"][:], io["x"].rearrange("(p b) d -> p (b d)", b=NB)).then_inc(x_loaded, 16)
            for name in ("ident", "w0", "w12", "bias0", "w1x", "w1e", "w2", "b2", "w3xa", "w3u", "b3", "w4", "u0"):
                sp.dma_start(mem[name][:], io[name]).then_inc(w_loaded, 16)
            sp.wait_ge(dve, marks["least_i"])
            sp.dma_start(io["scratch_base"].rearrange("(q c) -> q c", c=4), least_i[:]).then_inc(spread, 16)
            sp.wait_ge(spread, 16)
            sp.dma_start(mem["base_row0"][:], io["scratch_base"].rearrange("(a g) -> a g", a=1)).then_inc(spread, 16)
            sp.dma_start(base_bi[:], io["scratch_base"].rearrange("(a g) -> a g", a=1).broadcast_to([P, G])).then_inc(spread, 16)
            for k, (a, b) in enumerate(plan.slices):
                sp.wait_ge(table_ready, k + 1)
                sp.dma_start(io["table0"].rearrange("(p b) d -> p b d", b=NB)[:, a:b, :], stage[:, a:b, :]).then_inc(table_out, 16)
            sp.wait_ge(table_out, 16 * len(plan.slices))
            sp.wait_ge(w_loaded, 16 * 13)
            sp.wait_ge(spread, 48)

        @block.gpsimd
        def _(pool):
            pool.iota(iota_i[:], [[1, P]], base=0, channel_multiplier=0).then_inc(iota_ready, 1)
            pool.iota(iota_head, [[1, NB * plan.HW]], base=0, channel_multiplier=0).then_inc(iota_ready, 1)
            pool.wait_ge(iota_ready, 2)

        @block.scalar
        def _(act):
            act.wait_ge(dve, marks["deg_max"])
            act.activation(tmp2[:], tmp[:], ACT.Sqrt).then_inc(scaled, 1)

        @block.tensor
        def _(pe):
            def turn(n, k, start, stop):
                pe.wait_ge(hot_ready, n + 1)
                for u in range(U):
                    mm = pe.matmul(deg_ps[:, 0:NB], one_hi[:, k, :, u], one_lo[:, k, :, u],
                                   start=start and u == 0, stop=stop and u == U - 1)
                mm.then_inc(hot_used, 1)

            n_hot = T // U
            for k in range(HB):
                turn(k, k, k == 0, False)
            third = n_hot // HB // 3
            for a, b in ((1, third), (third, n_hot // HB - 1)):
                with pe.Fori(a, b) as i:
                    for k in range(HB):
                        turn(i * HB + k, k, False, False)
                if a == 1:
                    pe.wait_ge(w_loaded, 16 * 13)
                    pe.wait_ge(dve, marks["least"])
                    for c in range(4):
                        tr = pe.transpose(tr_ps[0:GC, c * P:(c + 1) * P], least[:].rearrange("p (q c) -> p c q", c=4)[:, c, :], mem["ident"][:])
                    tr.then_inc(turned, 1)
            for k in range(HB):
                turn(n_hot - HB + k, k, False, k == HB - 1)
            pe.wait_ge(dve, marks["far"])
            for k in range(6):
                tr = pe.transpose(tr_ps[0:1, k * P:(k + 1) * P], far[:, k:k + 1], mem["ident"][:])
            tr.then_inc(turned, 1)


class Side:

    region = None

    def attach(self, ctx, nc, plan, mem, io, tag, low, table):
        self.plan, self.mem, self.io, self.low, self.table = plan, mem, io, low, table
        self.first, self.last = 0, plan.CHUNKS
        self.peeled = []
        name = tag + type(self).__name__ + (f"{self.region.turn}_" if self.region else "_")
        sb = lambda n, s, d=F32: ctx.enter_context(nc.sbuf_tensor(name + n, s, d))
        sem = lambda n: ctx.enter_context(nc.semaphore(name + n))
        self.place(sb, lambda n: ctx.enter_context(nc.psum_tensor(name + n, [P, 512], F32)), sem)

    def place(self, sb, ps, sem):
        pass

    def blocks(self, name, c):
        p = self.plan
        return self.mem[name][:].rearrange("p (b d) -> p b d", d=p.D)[:, ds(c * p.CB, p.CB), :]

    def row(self, a):
        p = self.plan
        return a[0:p.NP, :].unsqueeze(1).broadcast_to([p.NP, p.CB, p.D])

    def wide(self, name, c):
        p = self.plan
        return self.mem[name][:, ds(c * p.CB, p.CB)].unsqueeze(2).broadcast_to([p.NP, p.CB, p.D])

    def flat(self, bank):
        p = self.plan
        return bank[0:p.NP, 0:p.CB * p.D].rearrange("p (b d) -> p b d", d=p.D)

    def sync(self, sp, c, slot):
        pass

    def scalar(self, act, c, slot):
        pass

    def tensor(self, pe, c, slot):
        pass

    def vector(self, v, c, slot):
        pass

    def early(self, v, c, slot):
        pass


class OwnPart(Side):

    def place(self, sb, ps, sem):
        p = self.plan
        self.x_t = sb("x_t", [p.D, p.CB, p.NP])
        self.own_ps = ps("own_ps")
        self.x_in, self.mixed, self.added = (sem(n) for n in ("x_in", "mixed", "added"))

    def sync(self, sp, c, slot):
        if slot == 0:
            wait_apart(sp, self.mixed, c, self.mem["passed"])
            chunk = self.io["x_t"].rearrange("f (b p) -> f b p", p=self.plan.NP)[:, ds(c * self.plan.CB, self.plan.CB), :]
            sp.dma_start(self.x_t[:], chunk).then_inc(self.x_in, 16)

    def tensor(self, pe, c, slot):
        D, NP = self.plan.D, self.plan.NP
        if slot == 0:
            wait(pe, self.added, c)
            pe.wait_ge(self.x_in, c * 16 + 16)
            for b in range(self.plan.CB):
                mm = pe.matmul(self.own_ps[0:NP, b * D:(b + 1) * D], self.x_t[:, b, :], self.mem["w0"][:], start=True, stop=True)
            mm.then_inc(self.mixed, 1)

    def vector(self, v, c, slot):
        x = self.blocks("xr", c)
        if slot == 2:
            v.wait_ge(self.mixed, c + 1)
            v.tensor_tensor(x, x, self.flat(self.own_ps), ALU.add).then_inc(self.added, 1)
            v.wait_ge(self.added, c + 1)
            v.tensor_tensor(x, x, self.row(self.mem["bias0"]), ALU.add)


class FirstHopPart(Side):

    def place(self, sb, ps, sem):
        p = self.plan
        self.part = sb("part", [p.D, p.CB, p.NP])
        self.scaled_part = sb("scaled_part", [p.NP, p.CB, p.D])
        self.hop_ps = ps("hop_ps")
        self.picked, self.mixed, self.scaled, self.done = (sem(n) for n in ("picked", "mixed", "scaled", "done"))

    def scalar(self, act, c, slot):
        p = self.plan
        if slot == 0:
            wait(act, self.mixed, c)
            act.copy(self.part[:], self.mem["sums"][0:p.D, 0:p.N].rearrange("f (p b) -> f b p", b=p.NB)[:, ds(c * p.CB, p.CB), :]).then_inc(self.picked, 1)

    def tensor(self, pe, c, slot):
        D, NP = self.plan.D, self.plan.NP
        if slot == 0:
            wait(pe, self.scaled, c)
            pe.wait_ge(self.picked, c + 1)
            for b in range(self.plan.CB):
                mm = pe.matmul(self.hop_ps[0:NP, b * D:(b + 1) * D], self.part[:, b, :], self.mem["w12"][0:D], start=True, stop=True)
            mm.then_inc(self.mixed, 1)

    def vector(self, v, c, slot):
        x = self.blocks("xr", c)
        if slot == 2:
            v.wait_ge(self.mixed, c + 1)
            wait(v, self.done, c)
            v.tensor_tensor(self.scaled_part[:], self.flat(self.hop_ps), self.wide("norm", c), ALU.mult).then_inc(self.scaled, 1)
            v.wait_ge(self.scaled, c + 1)
            v.tensor_tensor(x, x, self.scaled_part[:], ALU.add).then_inc(self.done, 1)


class MeanBias(Side):

    def vector(self, v, c, slot):
        if slot == 0:
            v.tensor_tensor(self.blocks("add2", c), self.row(self.mem["b2"]), self.wide("some", c), ALU.mult)


class HeadCounts(Side):

    def __init__(self, region, after=None):
        self.region, self.after = region, after

    def place(self, sb, ps, sem):
        self.first, self.last = self.region.counted, self.region.whole
        self.peeled = [self.first + 2]
        self.cleared, self.hot_ready, self.hot_used, self.added, self.whole = (
            sem(n) for n in ("cleared", "hot_ready", "hot_used", "added", "whole"))

    def unit(self, c, slot):
        slots = self.region.slots
        return None if self.clears(c) or slot >= slots else (c - self.first - 1) * slots + slot

    def clears(self, c):
        return isinstance(c, int) and c == self.first

    def tensor(self, pe, c, slot):
        p, u, W = self.plan, self.unit(c, slot), self.region.width
        if u is None:
            return
        if isinstance(u, int) and u == 0 and self.after:
            pe.wait_ge(self.after.added, 1)
        wait(pe, self.added, u)
        cols = p.NB // 4 * W
        for t in range(p.TG):
            pe.wait_ge(self.hot_ready, u * p.TG + t + 1)
            for k in range(4):
                mm = pe.matmul(self.mem["banks"][0:p.NP, k, 0:cols], self.mem["hot_p"][:, t % 2, :], self.mem["hot_b"][:, t % 2, k * cols:(k + 1) * cols],
                               start=(t == 0), stop=(t == p.TG - 1))
            mm.then_inc(self.hot_used, 1)

    def vector(self, v, c, slot):
        p, u, m, W = self.plan, self.unit(c, slot), self.mem, self.region.width
        if self.clears(c):
            if slot == 0 and self.after:
                v.wait_ge(self.after.stored, 16 * self.after.chunks)
                v.wait_ge(self.after.multiplied, self.after.chunks)
            n = p.NB // p.SLOTS
            v.memset(m["counts"][:, slot * n:(slot + 1) * n].rearrange("p b n -> p (b n)").bitcast(F32), 0.0).then_inc(self.cleared, 1)
        if u is None:
            return
        for t in range(p.TG):
            wait(v, self.hot_used, u * p.TG + t - 1)
            at = ds(u * p.TG + t + self.region.tiles[0], 1)
            v.tensor_scalar(m["hot_p"][:, t % 2, :], m["iota_2"][:, 0:p.NP], m["head_p"][:, at], None, ALU.is_equal)
            v.tensor_scalar(m["hot_b"][:, t % 2, 0:p.NB * W], m["iota_2"][:, 0:p.NB * W], m["head_b"][:, at], None, ALU.is_equal).then_inc(self.hot_ready, 1)

    def early(self, v, c, slot):
        u = self.unit(c, slot)
        if u is not None and not (isinstance(u, int) and u == 0):
            self.add(v, u - 1)

    def add(self, v, u):
        p, W = self.plan, self.region.width
        if isinstance(u, int) and u == 0:
            v.wait_ge(self.cleared, p.SLOTS)
        first = v.value_load(self.mem["base_head"][0:1, ds(u + self.region.groups[0], 1)], min_val=0, max_val=p.HN)
        v.wait_ge(self.hot_used, (u + 1) * p.TG)
        wait(v, self.added, u)
        window = self.mem["counts"][:, :, ds(first, W)].rearrange("p (k b) w -> p k b w", k=4)
        v.tensor_tensor(window, window, self.mem["banks"][0:p.NP, :, 0:p.NB // 4 * W].rearrange("p k (b w) -> p k b w", w=W),
                        ALU.add).then_inc(self.added, 1)

    def finish(self, v):
        groups = self.region.turns * self.plan.GB
        self.add(v, groups - 1)
        v.wait_ge(self.added, groups)
        v.sem_inc(self.whole, 1)


class HeadProduct(Side):

    def __init__(self, region, counts=None, after=None, load=False, store=False):
        self.region, self.counts, self.after, self.load, self.store = region, counts, after, load, store

    def place(self, sb, ps, sem):
        p = self.plan
        self.chunks = p.NB // p.PB
        self.first = self.counts.last if self.counts else self.region.again
        self.last = self.first + p.PT
        self.peeled = [self.last - 1]
        self.loaded, self.steps, self.multiplied, self.sum_steps, self.turned, self.added = (
            sem(n) for n in ("loaded", "steps", "multiplied", "sum_steps", "turned", "added"))
        if self.store:
            self.stored = sem("stored")
        if self.load:
            self.counts_in = sem("counts_in")
        if self.counts:
            self.largest_steps = sem("largest_steps")

    def marks(self):
        return {self.first: self.begin, self.last: self.take, self.last + 1: self.finish}

    def chunk(self, c, slot):
        return (c - self.first) * 2 + slot // 2

    def begin(self, name, engine, turns):
        if name == "vector" and self.counts:
            self.counts.finish(engine)

    def scalar(self, act, c, slot):
        p, m = self.plan, self.mem
        if slot in (0, 2):
            q = self.chunk(c, slot)
            begins = isinstance(q, int) and q == 0
            if begins and self.after:
                act.wait_ge(self.after.steps, self.chunks * 5)
            wait(act, self.steps, q * 5)
            chunk = self.table.rearrange("(p b) d -> p b d", b=p.NB)[:, ds(q * p.PB, p.PB), :]
            act.dma_start(m["head_t"][:], chunk).then_inc(self.loaded, 16)
            counts, dram = m["counts"][:, ds(q * p.PB, p.PB)], self.io["counts"][:, ds(q * p.PB, p.PB)]
            if self.store and slot == 2:
                if isinstance(q, int) and q == 1:
                    act.wait_ge(self.counts.whole, 1)
                for k in (q - 1, q):
                    at = ds(k * p.PB, p.PB)
                    act.dma_start(self.io["counts"][:, at], m["counts"][:, at]).then_inc(self.stored, 16)
            if self.load:
                if begins:
                    act.wait_ge(self.after.multiplied, self.chunks)
                wait(act, self.counts_in, q * 16)
                act.dma_start(counts, dram).then_inc(self.counts_in, 16)

    def vector(self, v, c, slot):
        m = self.mem
        if slot in (0, 2):
            if self.counts:
                self.largest(v, self.chunk(c, slot))
            return
        q = self.chunk(c, slot)
        t, rest = m["head_t"], m["head_rest"]
        part = lambda s: m["head_parts"][:, :, s, :]
        v.wait_ge(self.loaded, q * 16 + 16)
        if isinstance(q, int) and q == 0 and self.after:
            v.wait_ge(self.after.multiplied, self.chunks)
        wait(v, self.multiplied, q)
        for k, (out, a, b) in enumerate(((part(0), t, None), (rest[:], t, part(0)), (part(1), rest, None),
                                         (t[:], rest, part(1)), (part(2), t, None))):
            ins = v.tensor_copy(out, a[:]) if b is None else v.tensor_tensor(out, a[:], b, ALU.subtract)
            ins.then_inc(self.steps, 1)
            v.wait_ge(self.steps, q * 5 + k + 1)

    def largest(self, v, q):
        p, most = self.plan, self.mem["head_most"]
        wait(v, self.largest_steps, q * 2)
        v.tensor_reduce(most[:, 1:2], self.mem["counts"][:, ds(q * p.PB, p.PB), :], AX.XY, ALU.max).then_inc(self.largest_steps, 1)
        v.wait_ge(self.largest_steps, q * 2 + 1)
        v.tensor_tensor(most[:, 0:1], most[:, 0:1], most[:, 1:2], ALU.max).then_inc(self.largest_steps, 1)

    def tensor(self, pe, c, slot):
        if slot in (0, 2):
            return
        p, q = self.plan, self.chunk(c, slot)
        begins = isinstance(q, int) and q == 0
        ends = isinstance(q, int) and q == self.chunks - 1
        if begins:
            if self.counts:
                pe.wait_ge(self.counts.whole, 1)
            if self.after:
                pe.wait_ge(self.after.added, 1)
        if self.load:
            pe.wait_ge(self.counts_in, q * 16 + 16)
        pe.wait_ge(self.steps, q * 5 + 5)
        for b in range(p.PB):
            for k in range(4):
                mm = pe.matmul(self.mem["banks"][0:p.HQ, k, 0:3 * p.D],
                               self.mem["counts"][:, ds(q * p.PB + b, 1), k * p.HQ:(k + 1) * p.HQ].rearrange("p a n -> p (a n)"),
                               self.mem["head_parts"][:, b].rearrange("p s d -> p (s d)"), start=begins and b == 0, stop=ends and b == p.PB - 1)
        mm.then_inc(self.multiplied, 1)

    def take(self, name, engine, turns):
        p, m = self.plan, self.mem
        if name == "vector":
            v = engine
            v.memset(m["head_tall"][:], 0.0).then_inc(self.sum_steps, 1)
            v.wait_ge(self.multiplied, self.chunks)
            v.wait_ge(self.sum_steps, 1)
            tall = m["head_tall"][:, :, self.low:self.low + p.D]
            part = lambda s: m["banks"][0:p.HQ, :, s * p.D:(s + 1) * p.D]
            v.tensor_copy(tall, part(2)).then_inc(self.sum_steps, 1)
            v.wait_ge(self.sum_steps, 2)
            v.tensor_tensor(tall, tall, part(1), ALU.add).then_inc(self.sum_steps, 1)
            v.wait_ge(self.sum_steps, 3)
            v.tensor_tensor(tall, tall, part(0), ALU.add).then_inc(self.sum_steps, 1)
        if name == "tensor":
            engine.wait_ge(self.sum_steps, 4)
            for k in range(4):
                tr = engine.transpose(m["banks"][:, 2, k * p.HQ:(k + 1) * p.HQ], m["head_tall"][:, k, :], m["ident"][0:p.HQ, 0:p.HQ])
            tr.then_inc(self.turned, 1)

    def finish(self, name, engine, turns):
        p = self.plan
        if name == "vector":
            v = engine
            v.wait_ge(self.turned, 1)
            v.wait_ge(self.mem["sum_done"], turns * p.GB - 1)
            o = self.region.origin
            at = self.mem["sums"][self.low:self.low + p.D, o:o + p.HN]
            v.tensor_tensor(at, at, self.mem["banks"][self.low:self.low + p.D, 2, 0:p.HN], ALU.add).then_inc(self.added, 1)
            v.wait_ge(self.added, 1)


class Decision:

    def __init__(self, ctx, nc, plan, mem, products):
        self.plan, self.mem, self.products = plan, mem, products
        self.flags = ctx.enter_context(nc.sbuf_tensor("head_flags", [1, 12], F32))
        self.most_turned, self.flag_steps = (ctx.enter_context(nc.semaphore("head_" + n)) for n in ("most_turned", "flag_steps"))

    def tensor(self, pe):
        p = self.plan
        for product in self.products:
            pe.wait_ge(product.largest_steps, product.chunks * 2)
        pe.wait_ge(self.products[-1].added, 1)
        pe.transpose(self.mem["banks"][0:1, 3, 0:p.NP], self.mem["head_most"][:, 0:1], self.mem["ident"][0:p.NP, 0:p.NP]).then_inc(self.most_turned, 1)

    def vector(self, v):
        p, f = self.plan, self.flags
        steps = [0]

        def link(ins):
            steps[0] += 1
            ins.then_inc(self.flag_steps, 1)
            v.wait_ge(self.flag_steps, steps[0])

        v.wait_ge(self.most_turned, 1)
        link(v.tensor_reduce(f[:, 2:3], self.mem["banks"][0:1, 3, 0:p.NP], AX.X, ALU.max))
        link(v.tensor_tensor(f[:, 3:9], self.mem["extremes"][:], self.mem["limits"][:, 0:6], ALU.is_ge))
        link(v.tensor_tensor(f[:, 9:10], f[:, 2:3], self.mem["limits"][:, 6:7], ALU.is_ge))
        link(v.tensor_reduce(f[:, 0:1], f[:, 3:10], AX.X, ALU.max))
        link(v.tensor_copy(f[:, 1:2], self.mem["passes_any"][:]))
        link(v.tensor_tensor(f[:, 2:3], f[:, 0:1], f[:, 1:2], ALU.mult))
        link(v.tensor_copy(self.mem["passes"][:], f[:, 2:3]))


def edge_sums(nc, plan, mem, io, tag, table, low, sides, edge_mlp=False):
    N, D, T, G, TG, GB, TH, WIN, TURNS = plan.N, plan.D, plan.T, plan.G, plan.TG, plan.GB, plan.TH, plan.WIN, plan.TURNS
    F = plan.H if edge_mlp else D
    HG = GB // 2
    skip = 0 if edge_mlp else plan.HT
    with ExitStack() as ctx:
        sb = lambda n, s, d: ctx.enter_context(nc.sbuf_tensor(tag + n, s, d))
        ps = lambda n, s, d: ctx.enter_context(nc.psum_tensor(tag + n, s, d))
        sem = lambda n: ctx.enter_context(nc.semaphore(tag + n))
        index = sb("index", [P, 2, TH], I32)
        rows = sb("rows", [P, GB, TG, F], F32)
        hot = sb("hot", [P, 4, TG, WIN], F32)
        base = sb("base", [1, G], I32)
        seg_ps = [ps(f"seg_ps{k}", [P, 512], F32) for k in range(2)]
        if edge_mlp:
            edges = sb("edges", [plan.FE, 2, TH * P], F32)
            pre = sb("pre", [P, 2, TG, F], F32)
            hid = sb("hid", [P, 2, TG, F], F32)
            emb_ps = [ps(f"emb_ps{k}", [P, 512], F32) for k in range(2)]

        rows_in = [sem(f"rows_in{k}") for k in range(GB)]
        index_in = [sem(f"index_in{h}") for h in range(2)]
        hot_ready = sem("hot_ready")
        seg_done = sem("seg_done")
        sum_done = sem("sum_done")
        if edge_mlp:
            edges_in = [sem(f"edges_in{h}") for h in range(2)]
            emb_done = sem("emb_done")
            pre_ready = sem("pre_ready")
            hid_ready = sem("hid_ready")
        start = sem("start")
        decided = sem("decided")
        pass_done = sem("pass_done")
        pass_open = sem("pass_open")
        passed = sem("passed")

        mem["sum_done"], mem["passed"] = sum_done, passed
        for side in sides:
            side.attach(ctx, nc, plan, mem, io, tag, low, table)
        products = [side for side in sides if isinstance(side, HeadProduct)]
        decision = Decision(ctx, nc, plan, mem, products) if products and products[0].counts else None
        STARTS = 3 if decision else 2
        block = ctx.enter_context(nc.Block())

        def passes(name, engine, turn, last=None, reset=None, undo=None):
            main = TURNS - skip
            marks = {}
            for product in products:
                marks |= product.marks()
            beside = {"sync": lambda side: side.sync, "scalar": lambda side: side.scalar, "tensor": lambda side: side.tensor,
                      "vector": lambda side: side.vector, "gpsimd": lambda side: lambda engine, m, slot: None}[name]
            cuts = {0, 1, 2, main - 1, main, *marks}
            for side in sides:
                cuts |= {side.first, side.first + 1, side.last, *side.peeled}
            cuts = sorted(cuts)
            for a, b in zip(cuts, cuts[1:]):
                if a in marks:
                    marks[a](name, engine, a)
                now = [side for side in sides if side.first <= a < side.last]

                def step(m):
                    def sides_at(slot, early=False):
                        for side in now:
                            (side.early if early else beside(side))(engine, m, slot)

                    turn(m + skip, m, m, sides_at)

                if b == a + 1:
                    step(a)
                else:
                    with engine.Fori(a, b) as m:
                        step(m)
            if last:
                last(TURNS - 1, main - 1, main - 1)
            if engine is nc.vector:
                engine.wait_ge(sum_done, main * GB)
                if decision:
                    decision.vector(engine)
                engine.sem_inc(decided, 1)
            else:
                if decision and engine is nc.tensor:
                    decision.tensor(engine)
                engine.wait_ge(decided, 1)
            n = engine.value_load(mem["passes"][0:1, 0:1], min_val=0, max_val=-(-N // WIN) + 1)
            with engine.If(n > 0):

                def opened(p):
                    if reset:
                        reset(p)
                    else:
                        wait_apart(engine, pass_open, p + 1, passed)

                opened(0)
                with engine.Fori(0, n) as p:
                    turn(0, p * TURNS + main, 0)
                    with engine.Fori(1, TURNS - 1) as i:
                        turn(i, p * TURNS + main + i, i)
                    turn(TURNS - 1, p * TURNS + main + TURNS - 1, TURNS - 1)
                    if last:
                        last(TURNS - 1, p * TURNS + main + TURNS - 1, TURNS - 1)
                    opened(p + 1)
                if undo:
                    undo(n)

        def met(engine, semaphore, count, m, r, apart=False):
            if isinstance(r, int) and count(r) <= 0:
                return
            if apart:
                wait_apart(engine, semaphore, count(m), passed)
            else:
                engine.wait_ge(semaphore, count(m))

        def nothing(slot, early=False):
            pass

        def pads(i, k):
            return max(0, min(TG, (i * GB + k + 1) * TG - plan.REAL)) if isinstance(i, int) else 0

        def rows_met(engine, i, k, r):
            if pads(i, k) < TG:
                met(engine, rows_in[k], lambda j: j * 16 * TG + 16 * (TG - pads(i, k)), r, r)

        @block.sync
        def _(sp):
            def turn(i, m, r, beside=nothing):
                for h in range(2):
                    for k in range(h * HG, h * HG + HG):
                        met(sp, rows_in[k], lambda j: j * 16 * TG, r, r, apart=True)
                    sp.dma_start(index[:, h, :], io["src"][ds(i * 2 + h, 1)].rearrange("a p t -> (a p) t")).then_inc(index_in[h], 16)
                    if edge_mlp:
                        met(sp, emb_done, lambda j: j * GB - GB + (h + 1) * HG, m, r, apart=True)
                        sp.dma_start(edges[:, h, :], io["edge_t"][ds(i * 2 + h, 1)].rearrange("a f e -> (a f) e")).then_inc(edges_in[h], 16)
                    beside(h * 2)

            passes("sync", sp, turn)

        @block.gpsimd
        def _(pool):
            def turn(i, m, r, beside=nothing):
                for h in range(2):
                    met(pool, index_in[h], lambda j: j * 16 + 16, m, r, apart=True)
                    for k in range(h * HG, h * HG + HG):
                        met(pool, pre_ready if edge_mlp else seg_done, lambda j: j * GB - GB + k + 1, m, r, apart=True)
                        for t in range(TG - pads(i, k)):
                            at = (k - h * HG) * TG + t
                            pool.indirect_dma_start(rows[:, k, t, :], None, table,
                                                    bass.IndirectOffsetOnAxis(ap=index[:, h, at:at + 1], axis=0)
                                                    ).then_inc(rows_in[k], 16)

            def reset(p):
                wait_apart(pool, pass_done, p + 1, passed)
                turns = TURNS - skip if isinstance(p, int) else TURNS
                landed = [16 * (turns * TG - pads(TURNS - 1, k)) for k in range(GB)]
                pool.inc_swdge_sem(rows_in, landed, mode="sub")
                pool.sem_inc(pass_open, 1)

            passes("gpsimd", pool, turn, reset=reset)

        @block.scalar
        def _(act):
            def turn(i, m, r, beside=nothing):
                for k in range(GB):
                    if edge_mlp:
                        met(act, pre_ready, lambda j: j * GB + k + 1, m, r)
                        met(act, seg_done, lambda j: j * GB + k - 1, m, r)
                        act.activation(hid[:, k % 2], pre[:, k % 2], ACT.Relu).then_inc(hid_ready, 1)
                    if k % 2 == 1:
                        beside(k // 2)

            passes("scalar", act, turn)

        @block.tensor
        def _(pe):
            def embed(m, r, k):
                if k % HG == 0:
                    met(pe, edges_in[k // HG], lambda j: j * 16 + 16, m, r)
                met(pe, pre_ready, lambda j: j * GB + k - 1, m, r)
                for t in range(TG):
                    at = ((k % HG) * TG + t) * P
                    mm = pe.matmul(emb_ps[k % 2][:, t * F:(t + 1) * F], edges[:, k // HG, at:at + P], mem["w1e"][:],
                                   start=True, stop=True)
                mm.then_inc(emb_done, 1)

            def segment(i, m, r, k):
                met(pe, hot_ready, lambda j: j * GB + k + 1, m, r)
                if edge_mlp:
                    met(pe, hid_ready, lambda j: j * GB + k + 1, m, r)
                else:
                    rows_met(pe, i, k, r)
                met(pe, sum_done, lambda j: j * GB + k - 1, m, r)
                for t in range(TG):
                    values = hid[:, k % 2, t, :] if edge_mlp else rows[:, k, t, :]
                    mm = pe.matmul(seg_ps[k % 2][low:low + F, 0:WIN], values, hot[:, k % 4, t, :], start=(t == 0), stop=(t == TG - 1))
                mm.then_inc(seg_done, 1)

            def turn(i, m, r, beside=nothing):
                for k in range(GB):
                    if not edge_mlp:
                        segment(i, m, r, k)
                    else:
                        embed(m, r, k)
                        if k > 0 or not isinstance(r, int) or r > 0:
                            segment(i, m, r, k - 1)
                    if k % 2 == 1:
                        beside(k // 2)

            passes("tensor", pe, turn, last=(lambda i, m, r: segment(i, m, r, GB - 1)) if edge_mlp else None)

        @block.vector
        def _(v):
            v.memset(mem["sums"][low:low + F, :], 0.0).then_inc(start, 1)
            v.tensor_copy(base[:], mem["base_row0"][:]).then_inc(start, 1)
            if decision:
                v.memset(mem["head_most"][:], 0.0).then_inc(start, 1)
            v.wait_ge(start, STARTS)

            def one_hot(i, m, r, k):
                met(v, seg_done, lambda j: j * GB + k - 3, m, r)
                v.tensor_tensor(hot[:, k % 4], mem["rel"][:, ds((i * GB + k) * TG, TG)].unsqueeze(2).broadcast_to([P, TG, WIN]),
                                mem["iota_f"][:, 0:WIN].unsqueeze(1).broadcast_to([P, TG, WIN]), ALU.is_equal).then_inc(hot_ready, 1)

            def add_parts(i, m, r, k):
                rows_met(v, i, k, r)
                met(v, emb_done, lambda j: j * GB + k + 1, m, r)
                met(v, hid_ready, lambda j: j * GB + k - 1, m, r)
                v.tensor_tensor(pre[:, k % 2], emb_ps[k % 2][:].rearrange("p (t f) -> p t f", f=F), rows[:, k], ALU.add).then_inc(pre_ready, 1)

            def add_sums(i, m, r, k):
                first = v.value_load(base[0:1, ds(i * GB + k, 1)], min_val=0, max_val=N)
                met(v, seg_done, lambda j: j * GB + k + 1, m, r)
                met(v, sum_done, lambda j: j * GB + k, m, r)
                window = mem["sums"][low:low + F, ds(first, WIN)]
                v.tensor_tensor(window, window, seg_ps[k % 2][low:low + F, 0:WIN], ALU.add).then_inc(sum_done, 1)

            def turn(i, m, r, beside=nothing):
                for k in range(GB):
                    one_hot(i, m, r, k)
                    if edge_mlp:
                        add_parts(i, m, r, k)
                    if k > 0 or not isinstance(r, int) or r > 0:
                        add_sums(i, m, r, k - 1)
                    beside(k // 2, early=k % 2 == 0)

            def reset(p):
                if isinstance(p, int):
                    v.memset(mem["sums"][low:low + F, :], 0.0).then_inc(start, 1)
                    v.wait_ge(start, STARTS + 1)
                else:
                    v.wait_ge(sum_done, p * G + (TURNS - skip) * GB)
                    v.tensor_scalar(mem["rel"][:], mem["rel"][:], -float(WIN), None, ALU.add).then_inc(start, 1)
                    v.tensor_scalar(base[:], base[:], WIN, N, ALU.add, ALU.min).then_inc(start, 1)
                    v.wait_ge(start, p * 2 + STARTS + 1)
                v.sem_inc(pass_done, 1)
                v.wait_ge(pass_open, p + 1)

            def undo(n):
                with v.Fori(0, n) as p:
                    v.tensor_scalar(mem["rel"][:], mem["rel"][:], float(WIN), None, ALU.add).then_inc(start, 1)
                    v.wait_ge(start, n * 2 + p + STARTS + 2)

            passes("vector", v, turn, last=lambda i, m, r: add_sums(i, m, r, GB - 1), reset=reset, undo=undo)


def over_chunks(engine, plan, step):
    assert plan.CHUNKS % 2 == 1
    for c in range(3):
        step(c, c % 2)
    with engine.Fori(1, plan.CHUNKS // 2) as j:
        step(j * 2 + 1, 1)
        step(j * 2 + 2, 0)


def second_table(nc, plan, mem, io):
    D, NB, NP, CB, CH = plan.D, plan.NB, plan.NP, plan.CB, plan.CHUNKS
    with ExitStack() as ctx:
        sem = lambda n: ctx.enter_context(nc.semaphore("t_" + n))
        part = [ctx.enter_context(nc.sbuf_tensor(f"t_part{q}", [D, CB, NP], F32)) for q in range(2)]
        rows_ps = [ctx.enter_context(nc.psum_tensor(f"t_rows_ps{q}", [P, 512], F32)) for q in range(2)]
        stage = ctx.enter_context(nc.sbuf_tensor("t_stage", [NP, NB, D], F32))
        picked, turned, scaled, out, passed = sem("picked"), sem("turned"), sem("scaled"), sem("out"), mem["chunks_passed"]
        block = ctx.enter_context(nc.Block())
        sums = mem["sums"][0:D, 0:plan.N].rearrange("f (p b) -> f b p", b=NB)

        @block.scalar
        def _(act):
            def step(c, q):
                wait(act, turned, c - 1)
                act.copy(part[q][:], sums[:, ds(c * CB, CB), :]).then_inc(picked, 1)

            over_chunks(act, plan, step)

        @block.tensor
        def _(pe):
            def step(c, q):
                wait(pe, scaled, c - 1)
                wait_apart(pe, picked, c + 1, passed)
                for b in range(CB):
                    tr = pe.transpose(rows_ps[q][0:NP, b * D:(b + 1) * D], part[q][:, b, :], mem["ident"][0:D, 0:D])
                tr.then_inc(turned, 1)

            over_chunks(pe, plan, step)

        @block.vector
        def _(v):
            def step(c, q):
                v.wait_ge(turned, c + 1)
                v.tensor_tensor(stage[:, ds(c * CB, CB), :], rows_ps[q][0:NP, 0:CB * D].rearrange("p (b d) -> p b d", d=D),
                                mem["norm2"][:, ds(c * CB, CB)].unsqueeze(2).broadcast_to([NP, CB, D]), ALU.mult).then_inc(scaled, 1)

            over_chunks(v, plan, step)

        @block.sync
        def _(sp):
            table = io["table1"].rearrange("(p b) d -> p b d", b=NB)
            for a, b in plan.slices:
                sp.wait_ge(scaled, -(-b // CB))
                sp.dma_start(table[:, a:b, :], stage[:, a:b, :]).then_inc(out, 16)
            sp.wait_ge(out, 16 * len(plan.slices))


class LayerNorm:

    def __init__(self, ctx, nc, plan, tag, a, sems, links):
        self.plan, self.a, self.links = plan, a, links
        ends = [e * plan.CB for e in plan.norm_ends]
        self.slices = list(zip([0, *ends], ends))
        n = len(ends)
        self.before, self.before_pool, self.before_last = (n, n - 1, 1) if tag == "s_" else (0, 0, 0)
        self.sq = ctx.enter_context(nc.sbuf_tensor(tag + "sq", [plan.NP, plan.NB, plan.D], F32))
        self.stat = ctx.enter_context(nc.sbuf_tensor(tag + "stat", [plan.NP, 7, plan.NB], F32))
        self.chain, self.centred, self.squared, self.var_ready, self.root_ready, self.rstd_ready, self.scaled, self.scaled_last = sems

    def link(self, v, ins):
        self.links[0] += 1
        ins.then_inc(self.chain, 1)
        v.wait_ge(self.chain, self.links[0])

    def wide(self, k, a, b):
        return self.stat[:, k, a:b].unsqueeze(2).broadcast_to([self.plan.NP, b - a, self.plan.D])

    def centre(self, v, k):
        a, b = self.slices[k]
        t, D = self.a[:, a:b, :], self.plan.D
        self.link(v, v.tensor_reduce(self.stat[:, 0, a:b], t, AX.X, ALU.add))
        self.link(v, v.tensor_scalar(self.stat[:, 1, a:b], self.stat[:, 0, a:b], -1.0 / D, None, ALU.mult))
        v.tensor_tensor(t, t, self.wide(1, a, b), ALU.add).then_inc(self.centred, 1)

    def variance(self, v, n):
        a, b = self.slices[n]
        v.wait_ge(self.squared, self.before + n + 1)
        self.link(v, v.tensor_reduce(self.stat[:, 2, a:b], self.sq[:, a:b, :], AX.X, ALU.add))
        v.tensor_scalar(self.stat[:, 3, a:b], self.stat[:, 2, a:b], 1.0 / self.plan.D, EPS, ALU.mult, ALU.add).then_inc(self.var_ready, 1)

    def rstd(self, v, n):
        a, b = self.slices[n]
        s = lambda k: self.stat[:, k, a:b]
        v.wait_ge(self.root_ready, self.before + n + 1)
        self.link(v, v.reciprocal(s(5), s(4)))
        self.link(v, v.tensor_tensor(s(6), s(5), s(5), ALU.mult))
        self.link(v, v.tensor_tensor(s(6), s(6), s(3), ALU.mult))
        self.link(v, v.tensor_scalar(s(6), s(6), -0.5, 1.5, ALU.mult, ALU.add))
        v.tensor_tensor(s(5), s(6), s(5), ALU.mult).then_inc(self.rstd_ready, 1)

    def vector_end(self, v):
        last = len(self.slices) - 1
        self.centre(v, last)
        self.rstd(v, last - 1)
        self.variance(v, last)
        self.rstd(v, last)
        self.scale_last(v)

    def scale_last(self, v):
        last = len(self.slices) - 1
        a, b = self.slices[last]
        v.wait_ge(self.rstd_ready, self.before + last + 1)
        v.tensor_tensor(self.a[:, a:b, :], self.a[:, a:b, :], self.wide(5, a, b), ALU.mult).then_inc(self.scaled_last, 1)

    def square(self, act, k):
        a, b = self.slices[k]
        act.wait_ge(self.centred, self.before + k + 1)
        act.activation(self.sq[:, a:b, :], self.a[:, a:b, :], ACT.Square).then_inc(self.squared, 1)

    def root(self, act, k):
        a, b = self.slices[k]
        act.wait_ge(self.var_ready, self.before + k + 1)
        act.activation(self.stat[:, 4, a:b], self.stat[:, 3, a:b], ACT.Sqrt).then_inc(self.root_ready, 1)

    def scalar_end(self, act):
        last = len(self.slices) - 1
        self.root(act, last - 1)
        self.square(act, last)
        self.root(act, last)

    def scale(self, pool, k):
        a, b = self.slices[k]
        pool.wait_ge(self.rstd_ready, self.before + k + 1)
        pool.tensor_tensor(self.a[:, a:b, :], self.a[:, a:b, :], self.wide(5, a, b), ALU.mult).then_inc(self.scaled, 1)
        pool.wait_ge(self.scaled, self.before_pool + k + 1)


def first_layer(nc, plan, mem, io):
    N, D, H, NB, NP, CB, CH = plan.N, plan.D, plan.H, plan.NB, plan.NP, plan.CB, plan.CHUNKS
    with ExitStack() as ctx:
        sb = lambda n, s: ctx.enter_context(nc.sbuf_tensor("f_" + n, s, F32))
        ps = lambda n: ctx.enter_context(nc.psum_tensor("f_" + n, [P, 512], F32))
        sem = lambda n: ctx.enter_context(nc.semaphore("f_" + n))
        part = [sb(f"part{q}", [P, CB, NP]) for q in range(2)]
        part_n = sb("part_n", [NP, CB, D])
        x1_t = [sb(f"x1_t{q}", [D + 1, CB, NP]) for q in range(2)]
        rows3 = [sb(f"rows3{q}", [NP, CB, H]) for q in range(2)]
        hop_ps, turn_ps, tab_ps = ([ps(f"{n}{q}") for q in range(2)] for n in ("hop_ps", "turn_ps", "tab_ps"))
        xr = mem["xr"][:].rearrange("p (b d) -> p b d", d=D)
        norm = LayerNorm(ctx, nc, plan, "f_", xr, *mem["norm_sems"])
        picked, mixed, scaled, summed, ones = sem("picked"), sem("mixed"), sem("scaled_hop"), sem("summed"), sem("ones")
        handed, turned, copied, tab_done, tab_ready, passed = sem("handed"), sem("turned"), sem("copied"), sem("tab_done"), sem("tab_ready"), mem["chunks_passed"]
        out = [sem(f"out{q}") for q in range(2)]
        x1_in = [sb(f"x1_in{q}", [NP, CB, D]) for q in range(2)]
        BEHIND = 16
        block = ctx.enter_context(nc.Block())
        sums = mem["sums"][D:2 * D, 0:N].rearrange("f (p b) -> f b p", b=NB)
        table = io["table2"].rearrange("(p b) h -> p b h", b=NB)

        @block.sync
        def _(sp):
            def step(c, q):
                wait_apart(sp, tab_ready, c + 1, passed)
                sp.dma_start(table[:, ds(c * CB, CB), :], rows3[q][:]).then_inc(out[q], 16)

            over_chunks(sp, plan, step)
            sp.wait_ge(out[0], 16 * (CH // 2 + 1))
            sp.wait_ge(out[1], 16 * (CH // 2))

        @block.gpsimd
        def _(pool):
            def step(c, q):
                wait(pool, turned, c - 1)
                pool.tensor_copy(x1_in[q][:], xr[:, ds(c * CB, CB), :]).then_inc(handed, 1)

            staggered(pool, plan, [(step, 0)], {0: lambda: norm.scale(pool, 0), 8: lambda: norm.scale(pool, 1),
                                                16: lambda: norm.scale(pool, 2),
                                                22: lambda: pool.wait_ge(norm.scaled_last, norm.before_last + 1)})

        @block.scalar
        def _(act):
            def pick(c, q):
                wait(act, mixed, c - 1)
                act.copy(part[q][D:2 * D], sums[:, ds(c * CB, CB), :]).then_inc(picked, 1)

            def copy(c, q):
                act.wait_ge(turned, c + 1)
                wait(act, tab_done, c - 1)
                act.copy(x1_t[q][0:D], turn_ps[q][0:D, 0:CB * NP].rearrange("f (b p) -> f b p", p=NP)).then_inc(copied, 1)

            staggered(act, plan, [(pick, 0), (copy, BEHIND)], {
                10: lambda: norm.square(act, 0), 12: lambda: norm.root(act, 0),
                18: lambda: norm.square(act, 1), 20: lambda: norm.root(act, 1),
                24: lambda: norm.square(act, 2), 26: lambda: norm.root(act, 2),
                28: lambda: norm.square(act, 3), 30: lambda: norm.root(act, 3)})

        @block.tensor
        def _(pe):
            def mix(c, q):
                wait(pe, scaled, c - 1)
                pe.wait_ge(picked, c + 1)
                for b in range(CB):
                    mm = pe.matmul(hop_ps[q][0:NP, b * D:(b + 1) * D], part[q][D:2 * D, b, :], mem["w12"][D:2 * D], start=True, stop=True)
                mm.then_inc(mixed, 1)

            def turn(c, q):
                wait(pe, copied, c - 1)
                wait_apart(pe, handed, c + 1, passed)
                for b in range(CB):
                    tr = pe.transpose(turn_ps[q][0:D, b * NP:(b + 1) * NP], x1_in[q][:, b, :], mem["ident"][0:NP, 0:NP])
                tr.then_inc(turned, 1)

            def tab(c, q):
                pe.wait_ge(copied, c + 1)
                wait(pe, tab_ready, c - 1)
                for b in range(CB):
                    mm = pe.matmul(tab_ps[q][0:NP, b * H:(b + 1) * H], x1_t[q][:, b, :], mem["w1x"][:], start=True, stop=True)
                mm.then_inc(tab_done, 1)

            pe.wait_ge(ones, 2)
            staggered(pe, plan, [(turn, BEHIND), (mix, 0), (tab, BEHIND + 1)])

        @block.vector
        def _(v):
            v.memset(x1_t[0][D:D + 1], 1.0).then_inc(ones, 1)
            v.memset(x1_t[1][D:D + 1], 1.0).then_inc(ones, 1)

            def step(c, q):
                at = ds(c * CB, CB)
                v.wait_ge(mixed, c + 1)
                wait(v, summed, c)
                v.tensor_tensor(part_n[:], hop_ps[q][0:NP, 0:CB * D].rearrange("p (b d) -> p b d", d=D),
                                mem["norm"][:, at].unsqueeze(2).broadcast_to([NP, CB, D]), ALU.mult).then_inc(scaled, 1)
                v.wait_ge(scaled, c + 1)
                v.tensor_tensor(xr[:, at, :], xr[:, at, :], part_n[:], ALU.add).then_inc(summed, 1)

            def centre(k):
                v.wait_ge(summed, plan.norm_ends[k])
                norm.centre(v, k)

            def copy(c, q):
                v.wait_ge(tab_done, c + 1)
                wait(v, out[q], (c - q) * 8)
                v.tensor_copy(rows3[q][:], tab_ps[q][0:NP, 0:CB * H].rearrange("p (b h) -> p b h", h=H)).then_inc(tab_ready, 1)

            staggered(v, plan, [(step, 0), (copy, BEHIND + 1)], {
                9: lambda: centre(0), 11: lambda: norm.variance(v, 0), 13: lambda: norm.rstd(v, 0),
                17: lambda: centre(1), 19: lambda: norm.variance(v, 1), 21: lambda: norm.rstd(v, 1),
                23: lambda: centre(2), 25: lambda: norm.variance(v, 2), 27: lambda: (centre(3), norm.rstd(v, 2)),
                29: lambda: norm.variance(v, 3), 31: lambda: (norm.rstd(v, 3), norm.scale_last(v))})


def second_layer(nc, plan, mem, io):
    N, D, H, NB, NP, CB, CH = plan.N, plan.D, plan.H, plan.NB, plan.NP, plan.CB, plan.CHUNKS
    with ExitStack() as ctx:
        sb = lambda n, s: ctx.enter_context(nc.sbuf_tensor("s_" + n, s, F32))
        ps = lambda n: ctx.enter_context(nc.psum_tensor("s_" + n, [P, 512], F32))
        sem = lambda n: ctx.enter_context(nc.semaphore("s_" + n))
        part = [sb(f"part{q}", [P, CB, NP]) for q in range(2)]
        cat = [sb(f"cat{q}", [NP, CB, 2 * D]) for q in range(2)]
        agg_n = sb("agg_n", [NP, CB, D])
        cat_t = [sb(f"cat_t{q}", [2 * D, CB, NP]) for q in range(2)]
        hid_t = [sb(f"hid_t{q}", [D + 1, CB, NP]) for q in range(2)]
        c3 = sb("c3", [D, 1])
        agg_ps, turn_ps, hid_ps, out_ps = ([ps(f"{n}{q}") for q in range(2)] for n in ("agg_ps", "turn_ps", "hid_ps", "out_ps"))
        xr = mem["xr"][:].rearrange("p (b d) -> p b d", d=D)
        norm = LayerNorm(ctx, nc, plan, "s_", xr, *mem["norm_sems"])
        picked, agg_done, agg_scaled, cat_ready, x1_ready = sem("picked"), sem("agg_done"), sem("agg_scaled"), sem("cat_ready"), sem("x1_ready")
        turned, copied, hid_done, hid_ready, mlp_done, summed = sem("turned"), sem("copied"), sem("hid_done"), sem("hid_ready"), sem("mlp_done"), sem("summed")
        c3_done, start, out, passed = sem("c3_done"), sem("start"), sem("out"), mem["chunks_passed"]
        block = ctx.enter_context(nc.Block())
        sums = mem["sums"][:, 0:N].rearrange("f (p b) -> f b p", b=NB)
        add2 = mem["add2"][:].rearrange("p (b d) -> p b d", d=D)
        out_dram = io["out"].rearrange("(p b) d -> p b d", b=NB)
        flat = lambda bank: bank[0:NP, 0:CB * D].rearrange("p (b d) -> p b d", d=D)

        @block.sync
        def _(sp):
            for k, (a, b) in enumerate(norm.slices):
                if k < len(norm.slices) - 1:
                    sp.wait_ge(norm.scaled, norm.before_pool + k + 1)
                else:
                    sp.wait_ge(norm.scaled_last, norm.before_last + 1)
                sp.dma_start(out_dram[:, a:b, :], xr[:, a:b, :]).then_inc(out, 16)
            sp.wait_ge(out, 16 * len(norm.slices))

        @block.gpsimd
        def _(pool):
            def step(c, q):
                wait(pool, turned, c - 1)
                pool.tensor_copy(cat[q][:, :, 0:D], xr[:, ds(c * CB, CB), :]).then_inc(x1_ready, 1)

            staggered(pool, plan, [(step, 0)], {18: lambda: norm.scale(pool, 0)})
            norm.scale(pool, 1)
            norm.scale(pool, 2)

        @block.scalar
        def _(act):
            act.wait_ge(start, 3)

            def pick(c, q):
                wait(act, agg_done, c - 1)
                act.copy(part[q][:], sums[:, ds(c * CB, CB), :]).then_inc(picked, 1)

            def copy(c, q):
                act.wait_ge(turned, c + 1)
                wait(act, hid_done, c - 1)
                act.copy(cat_t[q][:], turn_ps[q][:, 0:CB * NP].rearrange("f (b p) -> f b p", p=NP)).then_inc(copied, 1)

            def relu(c, q):
                act.wait_ge(hid_done, c + 1)
                wait(act, mlp_done, c - 1)
                act.activation(hid_t[q][0:D], hid_ps[q][0:D, 0:CB * NP].rearrange("f (b p) -> f b p", p=NP), ACT.Relu,
                               bias=c3[:]).then_inc(hid_ready, 1)

            staggered(act, plan, [(pick, 0), (relu, 3), (copy, 2)], {
                13: lambda: norm.square(act, 0), 15: lambda: norm.root(act, 0),
                21: lambda: norm.square(act, 1), 23: lambda: norm.root(act, 1),
                27: lambda: norm.square(act, 2)})
            norm.scalar_end(act)

        @block.tensor
        def _(pe):
            pe.matmul(out_ps[0][0:D, 0:1], mem["w3u"][:], mem["u0"][:], start=True, stop=True).then_inc(c3_done, 1)
            pe.wait_ge(start, 3)

            def agg(c, q):
                wait(pe, agg_scaled, c - 1)
                pe.wait_ge(picked, c + 1)
                for b in range(CB):
                    mm = pe.matmul(agg_ps[q][0:NP, b * D:(b + 1) * D], part[q][:, b, :], mem["w2"][:], start=True, stop=True)
                mm.then_inc(agg_done, 1)

            def turn(c, q):
                wait(pe, copied, c - 1)
                pe.wait_ge(x1_ready, c + 1)
                wait_apart(pe, cat_ready, c + 1, passed)
                for b in range(CB):
                    tr = pe.transpose(turn_ps[q][:, b * NP:(b + 1) * NP], cat[q][:, b, :], mem["ident"][0:NP, 0:NP])
                tr.then_inc(turned, 1)

            def hid(c, q):
                wait(pe, hid_ready, c - 1)
                pe.wait_ge(copied, c + 1)
                pe.matmul(hid_ps[q][0:D, 0:CB * NP], mem["w3xa"][:], cat_t[q][:].rearrange("f b p -> f (b p)"),
                          start=True, stop=True).then_inc(hid_done, 1)

            def mlp(c, q):
                wait(pe, summed, c - 1)
                pe.wait_ge(hid_ready, c + 1)
                for b in range(CB):
                    mm = pe.matmul(out_ps[q][0:NP, b * D:(b + 1) * D], hid_t[q][:, b, :], mem["w4"][:], start=True, stop=True)
                mm.then_inc(mlp_done, 1)

            staggered(pe, plan, [(mlp, 4), (hid, 3), (turn, 2), (agg, 1)])

        @block.vector
        def _(v):
            v.memset(hid_t[0][D:D + 1], 1.0).then_inc(start, 1)
            v.memset(hid_t[1][D:D + 1], 1.0).then_inc(start, 1)
            v.wait_ge(c3_done, 1)
            v.tensor_tensor(c3[:], out_ps[0][0:D, 0:1], mem["b3"][:], ALU.add).then_inc(start, 1)

            def agg(c, q):
                v.wait_ge(agg_done, c + 1)
                wait(v, cat_ready, c)
                v.tensor_tensor(agg_n[:], flat(agg_ps[q]), mem["inv"][:, ds(c * CB, CB)].unsqueeze(2).broadcast_to([NP, CB, D]),
                                ALU.mult).then_inc(agg_scaled, 1)
                wait(v, turned, c - 1)
                v.wait_ge(agg_scaled, c + 1)
                v.tensor_tensor(cat[q][:, :, D:2 * D], agg_n[:], add2[:, ds(c * CB, CB), :], ALU.add).then_inc(cat_ready, 1)

            def add(c, q):
                v.wait_ge(mlp_done, c + 1)
                v.wait_ge(x1_ready, c + 1)
                at = xr[:, ds(c * CB, CB), :]
                v.tensor_tensor(at, at, flat(out_ps[q]), ALU.add).then_inc(summed, 1)

            def centre(k):
                v.wait_ge(summed, plan.norm_ends[k])
                norm.centre(v, k)

            staggered(v, plan, [(add, 4), (agg, 1)], {
                12: lambda: centre(0), 14: lambda: norm.variance(v, 0), 16: lambda: norm.rstd(v, 0),
                20: lambda: centre(1), 22: lambda: norm.variance(v, 1), 24: lambda: norm.rstd(v, 1),
                26: lambda: centre(2), 28: lambda: norm.variance(v, 2)})
            v.wait_ge(summed, CH)
            norm.vector_end(v)


def staggered(engine, plan, stages, before=None):
    before = before or {}
    n = plan.CHUNKS
    cuts = set(before)
    for _, lag in stages:
        cuts |= {lag, lag + 1, lag + 2, lag + 3, lag + n}
    cuts = sorted(cuts)
    for a, b in zip(cuts, cuts[1:]):
        if a in before:
            before[a]()
        now = [(stage, lag) for stage, lag in stages if lag <= a < lag + n]

        def turn(t, number):
            for stage, lag in now:
                stage(t - lag, (number - lag) % 2)

        pairs = (b - a) // 2
        if pairs >= 2:
            with engine.Fori(0, pairs) as j:
                for k in range(2):
                    turn(j * 2 + a + k, a + k)
        else:
            pairs = 0
        for t in range(a + 2 * pairs, b):
            turn(t, t)


def build(nc, plan, io):
    N, D, NB, NP, T, G, H = plan.N, plan.D, plan.NB, plan.NP, plan.T, plan.G, plan.H
    HT = plan.HT * plan.TG * plan.GB
    F16 = mybir.dt.float16
    with ExitStack() as ctx:
        mem = {}

        def place(stack, *tensors, tag="m_"):
            for name, shape, dt in tensors:
                mem[name] = stack.enter_context(nc.sbuf_tensor(tag + name, shape, dt))

        place(
            ctx,
            ("xr", [NP, NB * D], F32),
            ("sums", [P, N + plan.WIN], F32),
            ("rel", [P, T], F32),
            ("base_row0", [1, G], I32),
            ("passes", [1, 1], I32), ("passes_any", [1, 1], I32),
            ("extremes", [1, 6], F32),
            ("limits", [1, 7], F32),
            ("iota_f", [P, P], F32),
            ("norm", [NP, NB], F32), ("norm2", [NP, NB], F32),
            ("inv", [NP, NB], F32), ("some", [NP, NB], F32),
            ("ident", [P, P], F32),
            ("w0", [D, D], F32), ("w12", [2 * D, D], F32), ("bias0", [P, D], F32),
            ("w1x", [D + 1, H], F32), ("w1e", [plan.FE, H], F32),
            ("w2", [H, D], F32), ("b2", [P, D], F32),
            ("w3xa", [2 * D, D], F32), ("w3u", [D, D], F32), ("b3", [D, 1], F32),
            ("w4", [D + 1, D], F32), ("u0", [D, 1], F32),
        )
        mem["norm_sems"] = ([ctx.enter_context(nc.semaphore("norm_" + n)) for n in (
            "chain", "centred", "squared", "var_ready", "root_ready", "rstd_ready", "scaled", "scaled_last")], [0])
        mem["chunks_passed"] = ctx.enter_context(nc.semaphore("chunks_passed"))
        with ExitStack() as hops:
            place(
                hops,
                ("head_p", [P, HT], F32), ("head_b", [P, HT], F32),
                ("base_head", [1, HT // plan.TG], I32),
                ("iota_2", [P, NB * plan.HW], F16),
            )
            prologue(nc, plan, mem, io)
            head_buffers = (
                ("head_t", [NP, plan.PB, D], F32), ("head_rest", [NP, plan.PB, D], F32),
                ("head_parts", [NP, plan.PB, 3, D], BF16),
                ("head_tall", [plan.HQ, 4, 2 * D], F32),
            )
            place(hops, ("counts", [NP, NB, plan.HN + plan.HW], BF16))
            a, b = plan.regions
            with ExitStack() as hop:
                mem["banks"] = hop.enter_context(nc.psum_tensor("banks1", [P, 4, 512], F32))
                place(hop, *head_buffers,
                      ("hot_b", [P, 2, NB * plan.HW], BF16),
                      ("hot_p", [P, 2, NP], BF16),
                      ("head_most", [NP, 2], F32))
                counts_a = HeadCounts(a)
                product_a = HeadProduct(a, counts_a, store=True)
                counts_b = HeadCounts(b, after=product_a)
                product_b = HeadProduct(b, counts_b, after=product_a)
                edge_sums(nc, plan, mem, io, "h1_", io["table0"], 0, [OwnPart(), counts_a, product_a, counts_b, product_b])
            second_table(nc, plan, mem, io)
            with ExitStack() as hop:
                mem["banks"] = hop.enter_context(nc.psum_tensor("banks2", [P, 4, 512], F32))
                place(hop, *head_buffers, tag="m2_")
                product_b = HeadProduct(b)
                product_a = HeadProduct(a, after=product_b, load=True)
                edge_sums(nc, plan, mem, io, "h2_", io["table1"], D, [FirstHopPart(), product_b, product_a])
        first_layer(nc, plan, mem, io)
        place(ctx, ("add2", [NP, NB * D], F32))
        edge_sums(nc, plan, mem, io, "e_", io["table2"], 0, [MeanBias()], edge_mlp=True)
        second_layer(nc, plan, mem, io)


def kernel(**inputs):
    import numpy as np
    import concourse.bacc as bacc
    from concourse.bass_utils import run_bass_kernel_spmd

    x, src, dst, edge = (np.asarray(inputs[k]) for k in ("x", "src", "dst", "edge_attr_32"))
    w, b0, u, w3 = (np.asarray(inputs[k]) for k in ("L0_gnn_weight", "L0_gnn_bias", "L1_gnn_u", "L1_gnn_W3"))
    w1, b1, w2, b2, b3, w4, b4 = (np.asarray(inputs["L1_gnn_" + k]) for k in ("W1", "b1", "W2", "b2", "b3", "W4", "b4"))
    N, D = x.shape
    E, FE = edge.shape
    plan = Plan(N, E, D, FE, w1.shape[1])
    NB, NP, T, TH = plan.NB, plan.NP, plan.T, plan.TH
    pad = T * P - E
    src_p = np.concatenate([src, np.zeros(pad, src.dtype)])
    dst_p = np.concatenate([dst, np.full(pad, N, dst.dtype)])
    edge_p = np.concatenate([edge, np.zeros((pad, FE), edge.dtype)])
    rows = lambda a: np.ascontiguousarray(np.broadcast_to(a, (P, a.shape[0])))
    arrays = {
        "x": x,
        "x_t": x.reshape(NP, NB, D).transpose(2, 1, 0).reshape(D, N),
        "src": src_p.reshape(T // TH, TH, P).transpose(0, 2, 1),
        "dst": dst_p.reshape(T, P).T,
        "edge_t": edge_p.reshape(T // TH, TH * P, FE).transpose(0, 2, 1),
        "ident": np.eye(P, dtype=x.dtype),
        "w0": w[:, 0:D].T, "w12": w[:, D:3 * D].T, "bias0": rows(b0),
        "w1x": np.concatenate([w1[0:D], b1[None]]), "w1e": w1[D:D + FE],
        "w2": w2, "b2": rows(b2),
        "w3xa": w3[0:2 * D], "w3u": w3[2 * D:3 * D], "b3": b3[:, None],
        "w4": np.concatenate([w4, b4[None]]), "u0": u[0][:, None],
    }
    arrays = {"in_" + k: np.ascontiguousarray(a) for k, a in arrays.items()}
    nc = bacc.Bacc("TRN2", target_bir_lowering=False, num_devices=1)
    io = {k[3:]: nc.dram_tensor(k, a.shape, mybir.dt.from_np(a.dtype), kind="ExternalInput").ap() for k, a in arrays.items()}
    io["out"] = nc.dram_tensor("out_0", (N, D), F32, kind="ExternalOutput").ap()
    for name, shape, dt in (("table0", (N, D), F32), ("table1", (N, D), F32), ("table2", (N, plan.H), F32), ("scratch_base", (plan.G,), I32),
                            ("counts", (plan.NP, plan.NB, plan.HN + plan.HW), BF16)):
        io[name] = nc.dram_tensor(name, shape, dt, kind="Internal").ap()
    build(nc, plan, io)
    r = run_bass_kernel_spmd(nc, [arrays], core_ids=[0])
    return r.results[0]["out_0"]
```
